# Optimizing a Trainium2 kernel written in Bass

```python
import numpy as np
import jax
import jax.numpy as jnp

def _softmax(x, axis=-1):
    return jax.nn.softmax(x, axis=axis)

def _gelu(x):
    return jax.nn.gelu(x, approximate=True)

def _silu(x):
    return jax.nn.silu(x)

def _sigmoid(x):
    return jax.nn.sigmoid(x)

def _layernorm(x, axis=-1, eps=1e-05):
    m = jnp.mean(x, axis=axis, keepdims=True)
    v = jnp.var(x, axis=axis, keepdims=True)
    return (x - m) / jnp.sqrt(v + eps)

def _scatter_add(tgt, idx, src, axis=0):
    return tgt.at[idx].add(src)

def _segment_sum(src, seg, n):
    return jax.ops.segment_sum(src, seg, n)
kernel_name = 'mk_seq_preln_d1_jaxref_r8_125019'

def setup_inputs(seed: int=0):
    np.random.seed(seed)
    _w = jnp.asarray

    def _L0_attn_setup():
        import jax, jax.numpy as jnp
        import numpy as np
        B, S, HID = (1, 256, 512)
        NH, NKV = (32, 8)
        HD = HID // NH
        GROUPS = NH // NKV
        ROPE_THETA = 10000.0

        def _rope_cos_sin(seq_len, head_dim, dtype=jnp.float32):
            inv_freq = 1.0 / ROPE_THETA ** (jnp.arange(0, head_dim, 2, dtype=jnp.float32) / head_dim)
            t = jnp.arange(seq_len, dtype=jnp.float32)
            freqs = jnp.outer(t, inv_freq)
            emb = jnp.concatenate([freqs, freqs], axis=-1)
            return (jnp.cos(emb).astype(dtype), jnp.sin(emb).astype(dtype))

        def _rotate_half(x):
            x1, x2 = jnp.split(x, 2, axis=-1)
            return jnp.concatenate([-x2, x1], axis=-1)

        def _apply_rope(x, cos, sin):
            return x * cos[None, None] + _rotate_half(x) * sin[None, None]
        key = jax.random.key(seed)
        k1, k2, k3, k4, k5 = jax.random.split(key, 5)
        return {'hidden_states': jax.random.normal(k1, (B, S, HID), jnp.float32), 'Wq': jax.random.normal(k2, (NH * HD, HID), jnp.float32) * 0.02, 'Wk': jax.random.normal(k3, (NKV * HD, HID), jnp.float32) * 0.02, 'Wv': jax.random.normal(k4, (NKV * HD, HID), jnp.float32) * 0.02, 'Wo': jax.random.normal(k5, (HID, NH * HD), jnp.float32) * 0.02}
    _L0_attn_in = _L0_attn_setup()

    def _L0_ffn_setup():
        import jax, jax.numpy as jnp
        import numpy as np
        HIDDEN = 512
        INTER = 1376
        key = jax.random.key(seed)
        k0, k1, k2, k3 = jax.random.split(key, 4)
        scale_h = 1.0 / np.sqrt(HIDDEN)
        scale_i = 1.0 / np.sqrt(INTER)
        return {'x': jax.random.normal(k0, (4, 32, HIDDEN), dtype=jnp.float32), 'w_gate': jax.random.normal(k1, (INTER, HIDDEN), dtype=jnp.float32) * scale_h, 'w_up': jax.random.normal(k2, (INTER, HIDDEN), dtype=jnp.float32) * scale_h, 'w_down': jax.random.normal(k3, (HIDDEN, INTER), dtype=jnp.float32) * scale_i}
    _L0_ffn_in = _L0_ffn_setup()
    _d = {'L0_attn_hidden_states': _L0_attn_in['hidden_states'], 'L0_attn_Wq': _L0_attn_in['Wq'], 'L0_attn_Wk': _L0_attn_in['Wk'], 'L0_attn_Wv': _L0_attn_in['Wv'], 'L0_attn_Wo': _L0_attn_in['Wo'], 'L0_ffn_w_gate': _L0_ffn_in['w_gate'], 'L0_ffn_w_up': _L0_ffn_in['w_up'], 'L0_ffn_w_down': _L0_ffn_in['w_down']}
    _x0 = _d['L0_attn_hidden_states']
    _d['L0_attn_hidden_states'] = jax.random.normal(jax.random.fold_in(jax.random.key(seed), 1), (2, 1024, 512), dtype=_x0.dtype)
    del _x0
    return _d

def reference(L0_attn_hidden_states, L0_attn_Wq, L0_attn_Wk, L0_attn_Wv, L0_attn_Wo, L0_ffn_w_gate, L0_ffn_w_up, L0_ffn_w_down):

    def _L0_attn_ref(hidden_states, Wq, Wk, Wv, Wo):
        import jax, jax.numpy as jnp
        import numpy as np
        B, S, HID = (1, 256, 512)
        NH, NKV = (32, 8)
        HD = HID // NH
        GROUPS = NH // NKV
        ROPE_THETA = 10000.0

        def _rope_cos_sin(seq_len, head_dim, dtype=jnp.float32):
            inv_freq = 1.0 / ROPE_THETA ** (jnp.arange(0, head_dim, 2, dtype=jnp.float32) / head_dim)
            t = jnp.arange(seq_len, dtype=jnp.float32)
            freqs = jnp.outer(t, inv_freq)
            emb = jnp.concatenate([freqs, freqs], axis=-1)
            return (jnp.cos(emb).astype(dtype), jnp.sin(emb).astype(dtype))

        def _rotate_half(x):
            x1, x2 = jnp.split(x, 2, axis=-1)
            return jnp.concatenate([-x2, x1], axis=-1)

        def _apply_rope(x, cos, sin):
            return x * cos[None, None] + _rotate_half(x) * sin[None, None]
        bsz, q_len, _ = hidden_states.shape
        q = (hidden_states @ Wq.T).reshape(bsz, q_len, NH, HD).transpose(0, 2, 1, 3)
        k = (hidden_states @ Wk.T).reshape(bsz, q_len, NKV, HD).transpose(0, 2, 1, 3)
        v = (hidden_states @ Wv.T).reshape(bsz, q_len, NKV, HD).transpose(0, 2, 1, 3)
        cos, sin = _rope_cos_sin(q_len, HD, hidden_states.dtype)
        q = _apply_rope(q, cos, sin)
        k = _apply_rope(k, cos, sin)
        k = jnp.repeat(k, GROUPS, axis=1)
        v = jnp.repeat(v, GROUPS, axis=1)
        scale = 1.0 / jnp.sqrt(jnp.asarray(HD, hidden_states.dtype))
        logits = jnp.einsum('bhqd,bhkd->bhqk', q, k) * scale
        causal = jnp.tril(jnp.ones((q_len, q_len), dtype=bool))
        logits = jnp.where(causal[None, None], logits, jnp.finfo(logits.dtype).min)
        attn = jax.nn.softmax(logits, axis=-1)
        out = jnp.einsum('bhqk,bhkd->bhqd', attn, v)
        out = out.transpose(0, 2, 1, 3).reshape(bsz, q_len, NH * HD)
        return out @ Wo.T

    def _L0_ffn_ref(x, w_gate, w_up, w_down):
        import jax, jax.numpy as jnp
        import numpy as np
        HIDDEN = 512
        INTER = 1376
        gate = jax.nn.silu(jnp.einsum('bsh,ih->bsi', x, w_gate))
        up = jnp.einsum('bsh,ih->bsi', x, w_up)
        return jnp.einsum('bsi,hi->bsh', gate * up, w_down)
    x = L0_attn_hidden_states
    x = x + _L0_attn_ref(_layernorm(x, axis=-1), L0_attn_Wq, L0_attn_Wk, L0_attn_Wv, L0_attn_Wo)
    x = x + _L0_ffn_ref(_layernorm(x, axis=-1), L0_ffn_w_gate, L0_ffn_w_up, L0_ffn_w_down)
    return x

_drawn_inputs = setup_inputs


def setup_inputs(seed=0):
    import zlib

    import numpy as np

    out = dict(_drawn_inputs(seed))
    spreads = {}
    factors = {'L0_attn_Wq': 8.0, 'L0_attn_Wk': 8.0, 'L0_attn_Wv': 2.691, 'L0_attn_Wo': 2.788}
    for name, (base, spread) in spreads.items():
        noise = np.random.default_rng([zlib.crc32(name.encode()), seed]).standard_normal(out[name].shape)
        drawn = base * np.exp(spread * noise) if base else spread * noise
        out[name] = jnp.asarray(drawn.astype(out[name].dtype))
    for name, factor in factors.items():
        out[name] = (out[name] * factor).astype(out[name].dtype)
    return out
```

```python
from contextlib import ExitStack

import concourse.bass as bass
from concourse import mybir

ALU = mybir.AluOpType
ACT = mybir.ActivationFunctionType
F32 = mybir.dt.float32
F32R = mybir.dt.float32r
BF16 = mybir.dt.bfloat16

P = 128
HID = 512
KT = HID // P
BATCH, SEQ = 2, 1024
TOK = BATCH * SEQ
TT = TOK // P
ST = SEQ // P
NH, NKV = 32, 8
HD = HID // NH
GH = NH // NKV
QROWS, KROWS = NH * HD, NKV * HD
QK = QROWS + KROWS
QKV = QK + KROWS
QKT = QK // P
NG = BATCH * NKV
PARTS = 3
STACK = 6 * HD
STACKM = STACK + PARTS
INTER = 1376
IT = -(-INTER // P)
EPS = 1e-5
SCALE = HD ** -0.5
NEG = -3.0e38


def wait(engine, sem, value):
    if not (isinstance(value, int) and value <= 0):
        engine.wait_ge(sem, value)


def wait_apart(engine, sem, value, passed):
    if not (isinstance(value, int) and value <= 0):
        engine.wait_ge(sem, value)
        if not isinstance(value, int):
            engine.sem_inc(passed, 1)


def identity(engine, sem, tensor, n):
    engine.memset(tensor[:, :], 0.0).then_inc(sem, 1)
    engine.wait_ge(sem, n + 1)
    engine.affine_select(out=tensor[:, :], in_=tensor[:, :], compare_op=ALU.not_equal, fill=1.0, base=0,
                         pattern=[[-1, P]], channel_multiplier=1).then_inc(sem, 1)


def phase_a(nc, x, wqkv_t, cos_t, sin_t, q_parts, k_parts, v_all):
    with ExitStack() as ctx:
        def sb(name, shape, dt):
            return ctx.enter_context(nc.sbuf_tensor(name, shape, dt))

        def ps(name, shape):
            return ctx.enter_context(nc.psum_tensor(name, shape, F32))

        def sem(name):
            return ctx.enter_context(nc.semaphore(name))

        w_raw = sb("a_w_raw", [P, KT, QKV], F32)
        w_hi = sb("a_w_hi", [P, KT, QKV], F32R)
        w_lo = sb("a_w_lo", [P, KT, QKV], F32R)
        cos = sb("a_cos", [P, TT, HD], F32)
        sin = sb("a_sin", [P, TT, HD], F32)
        ident = sb("a_ident", [P, P], F32)
        x_in = sb("a_x_in", [P, 2, HID], F32)
        stats = sb("a_stats", [P, 2, 6], F32)
        mean_var = sb("a_mean_var", [P, 2, 2], F32)
        std = sb("a_std", [P, 2, 1], F32)
        rstd = sb("a_rstd", [P, 2, 1], F32)
        eps = sb("a_eps", [P, 1], F32)
        xn = sb("a_xn", [P, 2, HID], F32)
        xn_hi = sb("a_xn_hi", [P, 2, HID], F32R)
        xn_lo = sb("a_xn_lo", [P, 2, HID], F32R)
        by_cos = sb("a_by_cos", [P, 2, QK], F32)
        by_sin = sb("a_by_sin", [P, 2, QK], F32)
        roped = sb("a_roped", [P, 2, QK], F32)
        rest = sb("a_rest", [P, 2, QK], F32)
        parts = sb("a_parts", [P, PARTS, QKT, TOK], BF16)

        xt_ps = ps("a_xt_ps", [P, 2, HID])
        qkv_ps = ps("a_qkv_ps", [P, 2, 1024])
        rt_ps = ps("a_rt_ps", [P, 1024])

        weights_in = sem("a_weights_in")
        tables_in = sem("a_tables_in")
        x_loaded = [sem(f"a_x_loaded{s}") for s in range(2)]
        parts_out = sem("a_parts_out")
        pool_const = sem("a_pool_const")
        ones_set = sem("a_ones_set")
        w_hi_ready = sem("a_w_hi_ready")
        w_lo_ready = sem("a_w_lo_ready")
        stats_done = sem("a_stats_done")
        var_done = sem("a_var_done")
        std_done = sem("a_std_done")
        rstd_done = sem("a_rstd_done")
        xn_done = sem("a_xn_done")
        xt_done = sem("a_xt_done")
        xn_hi_done = sem("a_xn_hi_done")
        passed = sem("a_passed")
        xn_lo_done = sem("a_xn_lo_done")
        qkv_done = sem("a_qkv_done")
        cos_done = sem("a_cos_done")
        sin_done = sem("a_sin_done")
        v_done = sem("a_v_done")
        roped_done = sem("a_roped_done")
        rt_done = sem("a_rt_done")
        part0_done = sem("a_part0_done")
        rest_done = sem("a_rest_done")
        part1_done = sem("a_part1_done")
        part2_done = sem("a_part2_done")

        block = ctx.enter_context(nc.Block())

        def tok(t):
            return bass.ds(t * P, P)

        def tiles(engine, body, ahead=0):
            body(0, 0)
            body(1, 1)
            with engine.Fori(1, TT // 2 - 1) as pair:
                body(2 * pair, 0)
                body(2 * pair + 1, 1)
            body(TT - 2, 0)
            body(TT - 1, 1)

        @block.sync
        def _(sp):
            sp.dma_start(x_in[:, 0, :], x[0:P, :]).then_inc(x_loaded[0], 16)
            sp.dma_start(x_in[:, 1, :], x[P:2 * P, :]).then_inc(x_loaded[1], 16)
            sp.dma_start(w_raw[:, :, :], wqkv_t.rearrange("(k p) n -> p k n", p=P)).then_inc(weights_in, 16)
            for b in range(BATCH):
                sp.dma_start(cos[:, b * ST:(b + 1) * ST, :], cos_t.rearrange("(t p) d -> p t d", p=P)).then_inc(tables_in, 16)
                sp.dma_start(sin[:, b * ST:(b + 1) * ST, :], sin_t.rearrange("(t p) d -> p t d", p=P)).then_inc(tables_in, 16)

            def load(t, s):
                sp.wait_ge(xn_done, t - 1)
                sp.dma_start(x_in[:, s, :], x[tok(t), :]).then_inc(x_loaded[s], 16)

            def store(b):
                sp.wait_ge(part0_done, ST * (b + 1))
                sp.wait_ge(part1_done, ST * (b + 1))
                sp.wait_ge(part2_done, ST * (b + 1))
                for m in range(PARTS):
                    at = bass.ds(b * SEQ, SEQ)
                    sp.dma_start(q_parts[m, b * QROWS:(b + 1) * QROWS, :].rearrange("(c p) t -> p c t", p=P),
                                 parts[:, m, 0:QROWS // P, at]).then_inc(parts_out, 16)
                    sp.dma_start(k_parts[m, b * KROWS:(b + 1) * KROWS, :],
                                 parts[:, m, QROWS // P, at]).then_inc(parts_out, 16)

            with sp.Fori(1, TT // 2 - 2) as pair:
                load(2 * pair, 0)
                load(2 * pair + 1, 1)
            store(0)
            for t in range(TT - 4, TT):
                load(t, t % 2)
            store(1)
            sp.wait_ge(parts_out, 16 * 2 * PARTS * BATCH)

        @block.gpsimd
        def _(pool):
            identity(pool, pool_const, ident, 0)
            pool.memset(eps[:, :], EPS).then_inc(pool_const, 1)
            pool.memset(v_all[:, :, :, :], 1.0).then_inc(ones_set, 1)

            def add(t, s):
                pool.wait_ge(cos_done, t + 1)
                pool.wait_ge(sin_done, 2 * t + 2)
                wait(pool, rt_done, t - 1)
                pool.tensor_tensor(roped[:, s, :], by_cos[:, s, :], by_sin[:, s, :], ALU.add).then_inc(roped_done, 1)

            def last_part(t, s):
                pool.wait_ge(part1_done, t + 1)
                pool.tensor_tensor(parts[:, 2, :, tok(t)], rest[:, s, :].rearrange("p (c t) -> p c t", c=QKT),
                                   parts[:, 1, :, tok(t)], ALU.subtract).then_inc(part2_done, 1)

            add(0, 0)
            add(1, 1)
            last_part(0, 0)
            with pool.Fori(1, TT // 2) as pair:
                add(2 * pair, 0)
                last_part(2 * pair - 1, 1)
                add(2 * pair + 1, 1)
                last_part(2 * pair, 0)
            last_part(TT - 1, 1)

        @block.scalar
        def _(act):
            def std_of(t, s):
                act.wait_ge(var_done, t + 1)
                wait(act, rstd_done, t - 1)
                act.activation(std[:, s, :], mean_var[:, s, 1:2], ACT.Sqrt, bias=eps[:, :]).then_inc(std_done, 1)

            def hi(t, s):
                act.wait_ge(xt_done, t + 1)
                wait(act, qkv_done, t - 1)
                act.activation(xn_hi[:, s, :], xt_ps[:, s, :], ACT.Copy).then_inc(xn_hi_done, 1)

            def values(t, s):
                act.wait_ge(sin_done, 2 * t + 2)
                src = qkv_ps[:, s, QK:QKV].rearrange("p (g d) -> p g d", d=HD)
                act.activation(v_all[:, bass.ds(group_row(t), NKV), tile_of(t), 0:HD], src, ACT.Copy).then_inc(v_done, 1)

            def group_row(t):
                return (t // ST) * NKV

            def tile_of(t):
                return t % ST

            def first_parts(t, s):
                act.wait_ge(rt_done, t + 1)
                act.activation(parts[:, 0, :, tok(t)], rt_ps[:, 0:QK].rearrange("p (c t) -> p c t", c=QKT),
                               ACT.Copy).then_inc(part0_done, 1)

            def second_part(t, s):
                act.wait_ge(rest_done, t + 1)
                act.activation(parts[:, 1, :, tok(t)], rest[:, s, :].rearrange("p (c t) -> p c t", c=QKT),
                               ACT.Copy).then_inc(part1_done, 1)

            act.wait_ge(pool_const, 3)
            act.wait_ge(ones_set, 1)
            std_of(0, 0)
            act.wait_ge(weights_in, 16)
            for k in range(KT):
                act.activation(w_hi[:, k, :], w_raw[:, k, :], ACT.Copy).then_inc(w_hi_ready, 1)
            std_of(1, 1)
            hi(0, 0)
            std_of(2, 0)
            hi(1, 1)
            values(0, 0)
            std_of(3, 1)
            hi(2, 0)
            values(1, 1)
            first_parts(0, 0)
            second_part(0, 0)

            def step(t, s, more):
                if more:
                    std_of(t + 2, s)
                if more or s == 0:
                    hi(t + 1, 1 - s)
                values(t, s)
                first_parts(t - 1, 1 - s)
                second_part(t - 1, 1 - s)

            with act.Fori(1, TT // 2 - 1) as pair:
                step(2 * pair, 0, True)
                step(2 * pair + 1, 1, True)
            step(TT - 2, 0, False)
            step(TT - 1, 1, False)
            first_parts(TT - 1, 1)
            second_part(TT - 1, 1)

        @block.vector
        def _(dve):
            def moments(t, s):
                if isinstance(t, int):
                    dve.wait_ge(x_loaded[s], 16 * (t // 2 + 1))
                else:
                    dve.wait_ge(x_loaded[s], 8 * (t - s) + 16)
                wait(dve, std_done, t - 1)
                wait(dve, xn_done, t - 1)
                dve.bn_stats(stats[:, s, :], x_in[:, s, :]).then_inc(stats_done, 1)
                wait_apart(dve, stats_done, t + 1, passed)
                dve.bn_aggr(mean_var[:, s, :], stats[:, s, :]).then_inc(var_done, 1)

            def normalise(t, s):
                dve.wait_ge(std_done, t + 1)
                dve.reciprocal(rstd[:, s, :], std[:, s, :]).then_inc(rstd_done, 1)
                dve.wait_ge(rstd_done, t + 1)
                wait(dve, xt_done, t - 1)
                dve.tensor_scalar(xn[:, s, :], x_in[:, s, :], mean_var[:, s, 0:1], rstd[:, s, :],
                                  ALU.subtract, ALU.mult).then_inc(xn_done, 1)

            def lo(t, s):
                dve.wait_ge(xn_hi_done, t + 1)
                dve.tensor_tensor(xn_lo[:, s, :], xt_ps[:, s, :], xn_hi[:, s, :].bitcast(F32),
                                  ALU.subtract).then_inc(xn_lo_done, 1)

            def rotate(t, s):
                dve.wait_ge(qkv_done, t + 1)
                wait(dve, roped_done, t - 1)
                heads = qkv_ps[:, s, 0:QK].rearrange("p (h d) -> p h d", d=HD)
                n = NH + NKV
                dve.tensor_tensor(by_cos[:, s, :].rearrange("p (h d) -> p h d", d=HD), heads,
                                  cos[:, bass.ds(t, 1), :].to_broadcast([P, n, HD]),
                                  ALU.mult).then_inc(cos_done, 1)
                to = by_sin[:, s, :].rearrange("p (h d) -> p h d", d=HD)
                half = HD // 2
                for a, b in ((0, half), (half, 0)):
                    dve.tensor_tensor(to[:, :, a:a + half], heads[:, :, b:b + half],
                                      sin[:, bass.ds(t, 1), a:a + half].to_broadcast([P, n, half]),
                                      ALU.mult).then_inc(sin_done, 1)

            def remainder(t, s):
                dve.wait_ge(part0_done, t + 1)
                wait(dve, part2_done, t - 1)
                wait(dve, part1_done, t - 1)
                dve.tensor_tensor(rest[:, s, :].rearrange("p (c t) -> p c t", c=QKT),
                                  rt_ps[:, 0:QK].rearrange("p (c t) -> p c t", c=QKT),
                                  parts[:, 0, :, tok(t)], ALU.subtract).then_inc(rest_done, 1)

            moments(0, 0)
            moments(1, 1)
            normalise(0, 0)
            for k in range(KT):
                dve.wait_ge(w_hi_ready, k + 1)
                dve.tensor_tensor(w_lo[:, k, :], w_raw[:, k, :], w_hi[:, k, :].bitcast(F32),
                                  ALU.subtract).then_inc(w_lo_ready, 1)
            normalise(1, 1)
            lo(0, 0)
            dve.wait_ge(tables_in, 64)
            moments(2, 0)
            lo(1, 1)
            normalise(2, 0)
            rotate(0, 0)
            moments(3, 1)
            lo(2, 0)
            normalise(3, 1)
            rotate(1, 1)
            remainder(0, 0)

            def step(t, s, more):
                if more:
                    moments(t + 2, s)
                if more or s == 0:
                    lo(t + 1, 1 - s)
                if more:
                    normalise(t + 2, s)
                rotate(t, s)
                remainder(t - 1, 1 - s)

            with dve.Fori(1, TT // 2 - 1) as pair:
                step(2 * pair, 0, True)
                step(2 * pair + 1, 1, True)
            step(TT - 2, 0, False)
            step(TT - 1, 1, False)
            remainder(TT - 1, 1)

        @block.tensor
        def _(pe):
            def x_transposes(t, s):
                pe.wait_ge(xn_done, t + 1)
                wait(pe, xn_lo_done, t - 1)
                for k in range(KT):
                    mm = pe.transpose(xt_ps[:, s, k * P:(k + 1) * P], xn[:, s, k * P:(k + 1) * P], ident[:, :])
                mm.then_inc(xt_done, 1)

            def products(t, s):
                pe.wait_ge(xn_hi_done, t + 1)
                pe.wait_ge(xn_lo_done, t + 1)
                wait(pe, v_done, t - 1)
                wait(pe, cos_done, t - 1)
                wait(pe, sin_done, 2 * t - 2)
                for c0, c1 in ((0, QROWS), (QROWS, QKV)):
                    n = 0
                    for k in range(KT):
                        for a, w in ((xn_hi, w_hi), (xn_hi, w_lo), (xn_lo, w_hi)):
                            mm = pe.matmul(qkv_ps[:, s, c0:c1], a[:, s, k * P:(k + 1) * P], w[:, k, c0:c1],
                                           start=(n == 0), stop=(n == 3 * KT - 1))
                            n += 1
                mm.then_inc(qkv_done, 1)

            def r_transposes(t, s):
                pe.wait_ge(roped_done, t + 1)
                wait(pe, rest_done, t)
                for c in range(QKT):
                    mm = pe.transpose(rt_ps[:, c * P:(c + 1) * P], roped[:, s, c * P:(c + 1) * P], ident[:, :])
                mm.then_inc(rt_done, 1)

            pe.wait_ge(pool_const, 2)
            x_transposes(0, 0)
            pe.wait_ge(w_lo_ready, KT)
            x_transposes(1, 1)
            products(0, 0)
            x_transposes(2, 0)
            products(1, 1)
            r_transposes(0, 0)
            with pe.Fori(1, TT // 2 - 1) as pair:
                for s in range(2):
                    t = 2 * pair + s
                    x_transposes(t + 1, 1 - s)
                    products(t, s)
                    r_transposes(t - 1, 1 - s)
            x_transposes(TT - 1, 1)
            products(TT - 2, 0)
            r_transposes(TT - 3, 1)
            products(TT - 1, 1)
            r_transposes(TT - 2, 0)
            r_transposes(TT - 1, 1)


def phase_b(nc, q_parts, k_parts, v_all, o_rows):
    UNITS = GH * ST
    AHEAD = 6
    TURN = 2
    SLOTS = 3
    HALF = SEQ // 2
    CHUNKS = [(hf, j) for hf in range(2) for j in range((hf + 1) * ST // 2)]
    NC = len(CHUNKS)
    DIAG = [c for c, (hf, j) in enumerate(CHUNKS) if j * P >= hf * HALF]
    PRING = 4

    class At:
        def __init__(self, p, k):
            self.p, self.k = p, k
            self.n, self.slot, self.turn = SLOTS * p + k, k % SLOTS, p + k // SLOTS

        def next(self, by=1):
            return At(self.p, self.k + by)

        def has(self, by=1):
            return not isinstance(self.n, int) or self.n + by < NG

    def start_of(c):
        hf, j = CHUNKS[c]
        q0 = max(hf * HALF, j * P)
        return q0, (hf + 1) * HALF - q0

    def unit_of(u):
        return ST - 1 - u // GH, u % GH

    def plan():
        events = [("u", 1, u) for u in range(AHEAD, UNITS)]
        events += [("u", 2, u) for u in range(TURN)] + [("t", 1, 0)] + [("u", 2, u) for u in range(TURN, AHEAD)]
        cost = [P * (unit_of(u)[0] + 1) + 60 if kind == "u" else P for kind, _, u in events]
        work = [start_of(c)[1] for c in range(NC) for _ in range(GH)]
        out, e, done, made = [], 0, 0, 0
        for wk in work:
            made += wk
            here = []
            while e < len(events) and (done + cost[e] / 2) * sum(work) <= made * sum(cost):
                here.append(events[e])
                done += cost[e]
                e += 1
            out.append(here)
        out[-1] += events[e:]
        return out

    PLAN = plan()
    TURN_AT = next(i for i, here in enumerate(PLAN) if ("t", 1, 0) in here)

    def over_groups(engine, step):
        step(At(0, 0))
        with engine.Fori(0, (NG - 4) // SLOTS) as p:
            for k in range(1, SLOTS + 1):
                step(At(p, k))
        for n in range(NG - 3, NG):
            step(At(n // SLOTS, n % SLOTS))

    with ExitStack() as ctx:
        def sb(name, shape, dt):
            return ctx.enter_context(nc.sbuf_tensor(name, shape, dt))

        def ps(name, shape, dt=F32):
            return ctx.enter_context(nc.psum_tensor(name, shape, dt))

        def sem(name):
            return ctx.enter_context(nc.semaphore(name))

        q_stack = [sb(f"b_q_stack{s}", [P, GH, SEQ], BF16) for s in range(SLOTS)]
        k_stack = [sb(f"b_k_stack{s}", [P, SEQ], BF16) for s in range(SLOTS)]
        v_here = [sb(f"b_v_here{s}", [P, ST, 2 * HD], F32) for s in range(SLOTS)]
        probs = sb("b_probs", [P, PRING, GH, HALF], F32)
        mask = sb("b_mask", [P, SEQ], BF16)
        future = sb("b_future", [P, P], BF16)
        ident = sb("b_ident", [P, P], BF16)
        masked = sb("b_masked", [P, 4, SEQ], BF16)
        maxima = sb("b_maxima", [P, SLOTS, UNITS], F32)
        max_rest = sb("b_max_rest", [P, 2, UNITS], F32)
        neg_max = sb("b_neg_max", [P, PARTS, UNITS], BF16)
        neg_max_t = sb("b_neg_max_t", [PARTS * UNITS, P], BF16)
        o_sb = sb("b_o_sb", [P, 2, HALF], F32)

        max_ps = ps("b_max_ps", [P, 2, SEQ])
        exp_ps = ps("b_exp_ps", [P, 2, HALF])
        o_ps = ps("b_o_ps", [P, 2, HALF])
        turn_ps = max_ps[0:PARTS * UNITS, 0, 0:P // 2].bitcast(BF16)

        ones_set = sem("b_ones_set")
        mask_set = sem("b_mask_set")
        ident_set = sem("b_ident_set")
        stack_in = [sem(f"b_stack_in{s}") for s in range(SLOTS)]
        scores_max = sem("b_scores_max")
        max_read = sem("b_max_read")
        neg_done = sem("b_neg_done")
        turned = sem("b_turned")
        turn_copied = sem("b_turn_copied")
        neg_in = sem("b_neg_in")
        scores_exp = sem("b_scores_exp")
        exp_done = sem("b_exp_done")
        pv_done = sem("b_pv_done")
        o_copied = sem("b_o_copied")
        dve_passed = sem("b_dve_passed")
        pool_passed = sem("b_pool_passed")
        o_stored = [sem(f"b_o_stored{s}") for s in range(2)]

        block = ctx.enter_context(nc.Block())
        LOADS = 2 * PARTS * (PARTS + 1) // 2 + 1
        SPLIT = 5

        @block.sync
        def _(sp):
            def load(g):
                done = stack_in[g.slot]
                rows = 0
                for m in range(PARTS):
                    copies = PARTS - m
                    for r in range(copies):
                        sp.dma_start(q_stack[g.slot][rows + r * HD:rows + (r + 1) * HD, :, :],
                                     q_parts[m, bass.ds(g.n * GH * HD, GH * HD), :].rearrange("(h d) t -> d h t", d=HD)
                                     ).then_inc(done, 16)
                        sp.dma_start(k_stack[g.slot][rows + r * HD:rows + (r + 1) * HD, :],
                                     k_parts[r, bass.ds(g.n * HD, HD), :]).then_inc(done, 16)
                    rows += copies * HD
                sp.dma_start(v_here[g.slot][:, :, :], v_all[:, bass.ds(g.n, 1), :, :].rearrange("p a j d -> p (a j) d")
                             ).then_inc(done, 16)

            def neg_rows(g):
                sp.wait_ge(turn_copied, g.n + 1)
                for m in range(PARTS):
                    sp.dma_start(q_stack[g.slot][STACK + m:STACK + m + 1, :, :].rearrange("m h (i t) -> m (h i) t", t=P),
                                 neg_max_t[m * UNITS:(m + 1) * UNITS, :]).then_inc(neg_in, 16)

            def store(g, hf):
                sp.wait_ge(o_copied, 2 * g.n + hf + 1)
                sp.dma_start(o_rows[bass.ds(g.n, 1), :, hf * HALF:(hf + 1) * HALF].rearrange("a p t -> (a p) t"),
                             o_sb[:, hf, :]).then_inc(o_stored[hf], 16)

            def step(g):
                if g.has(2):
                    wait(sp, pv_done, NC * g.n)
                    load(g.next(2))
                if not (isinstance(g.n, int) and g.n == 0):
                    store(g.next(-1), 1)
                store(g, 0)
                if g.has(1):
                    neg_rows(g.next(1))

            load(At(0, 0))
            load(At(0, 1))
            neg_rows(At(0, 0))
            over_groups(sp, step)
            store(At(0, NG - 1), 1)
            sp.wait_ge(o_stored[0], 16 * NG)
            sp.wait_ge(o_stored[1], 16 * NG)

        @block.gpsimd
        def _(pool):
            for s in range(SLOTS):
                pool.memset(k_stack[s][STACK:STACKM, :], 1.0).then_inc(ones_set, 1)
            pool.wait_ge(ones_set, SLOTS)
            pool.memset(mask[:, :], 0.0).then_inc(mask_set, 1)
            pool.wait_ge(mask_set, 1)
            pool.affine_select(out=mask[:, SEQ - P:], in_=mask[:, SEQ - P:], compare_op=ALU.is_ge, fill=NEG, base=0,
                               pattern=[[-1, P]], channel_multiplier=1).then_inc(mask_set, 1)
            pool.memset(future[:, :], 0.0).then_inc(mask_set, 1)
            pool.wait_ge(mask_set, 3)
            pool.affine_select(out=future[:, :], in_=future[:, :], compare_op=ALU.is_ge, fill=NEG, base=0,
                               pattern=[[1, P]], channel_multiplier=-1).then_inc(mask_set, 1)
            identity(pool, ident_set, ident, 0)

            def split(g):
                mx, rs, ng = maxima[:, g.slot, :], max_rest, neg_max
                base = SPLIT * g.n
                pool.wait_ge(max_read, UNITS * (g.n + 1))
                wait_apart(pool, turned, g.n, pool_passed)
                pool.tensor_scalar(ng[:, 0, :], mx, -1.0, None, ALU.mult).then_inc(neg_done, 1)
                wait_apart(pool, neg_done, base + 1, pool_passed)
                pool.tensor_tensor(rs[:, 0, :], mx, ng[:, 0, :], ALU.add).then_inc(neg_done, 1)
                wait_apart(pool, neg_done, base + 2, pool_passed)
                pool.tensor_scalar(ng[:, 1, :], rs[:, 0, :], -1.0, None, ALU.mult).then_inc(neg_done, 1)
                wait_apart(pool, neg_done, base + 3, pool_passed)
                pool.tensor_tensor(rs[:, 1, :], rs[:, 0, :], ng[:, 1, :], ALU.add).then_inc(neg_done, 1)
                wait_apart(pool, neg_done, base + 4, pool_passed)
                pool.tensor_scalar(ng[:, 2, :], rs[:, 1, :], -1.0, None, ALU.mult).then_inc(neg_done, 1)

            split(At(0, 0))

            def step(g):
                if g.has(1):
                    split(g.next(1))

            over_groups(pool, step)

        @block.scalar
        def _(act):
            def copy_turn(g):
                act.wait_ge(turned, g.n + 1)
                wait(act, neg_in, 16 * PARTS * g.n)
                act.activation(neg_max_t[:, :], turn_ps, ACT.Copy).then_inc(turn_copied, 1)

            def copy_o(g, hf):
                act.wait_ge(pv_done, NC * g.n + (NC if hf else ST // 2))
                wait(act, o_stored[hf], 16 * g.n)
                act.activation(o_sb[:, hf, :], o_ps[:, hf, :], ACT.Copy).then_inc(o_copied, 1)

            def step(g):
                for c in range(NC):
                    q0, w = start_of(c)
                    for h in range(GH):
                        i = c * GH + h
                        act.wait_ge(scores_exp, GH * NC * g.n + i + 1)
                        if h == 0:
                            wait(act, pv_done, NC * g.n + c - PRING + 1)
                        act.activation(probs[:, c % PRING, h, 0:w], exp_ps[:, i % 2, 0:w], ACT.Exp,
                                       scale=SCALE).then_inc(exp_done, 1)
                        if i == TURN_AT and g.has(1):
                            copy_turn(g.next(1))
                    if c == 2 and not (isinstance(g.n, int) and g.n == 0):
                        copy_o(g.next(-1), 1)
                    if c == ST // 2 + 2:
                        copy_o(g, 0)

            copy_turn(At(0, 0))
            over_groups(act, step)
            copy_o(At(0, NG - 1), 1)

        @block.vector
        def _(dve):
            dve.wait_ge(mask_set, 2)

            def unit(g, u):
                i, h = unit_of(u)
                w = P * (i + 1)
                dve.wait_ge(scores_max, UNITS * g.n + u + 1)
                wait_apart(dve, max_read, UNITS * g.n + u - 3, dve_passed)
                dve.tensor_tensor_reduce(masked[:, u % 4, 0:w], max_ps[:, u % 2, 0:w], mask[:, SEQ - w:], 1.0, NEG,
                                         ALU.add, ALU.max, maxima[:, g.slot, h * ST + i:h * ST + i + 1]).then_inc(max_read, 1)

            for u in range(UNITS):
                unit(At(0, 0), u)
            for u in range(AHEAD):
                unit(At(0, 1), u)

            def step(g):
                for here in PLAN:
                    for kind, by, u in here:
                        if kind == "u" and g.has(by):
                            unit(g.next(by), u)

            over_groups(dve, step)

        @block.tensor
        def _(pe):
            def stacked(g):
                pe.wait_ge(stack_in[g.slot], 16 * LOADS * (g.turn + 1))

            def max_scores(g, u):
                i, h = unit_of(u)
                if u == 0:
                    stacked(g)
                wait(pe, max_read, UNITS * g.n + u - 1)
                if u == TURN:
                    wait(pe, turn_copied, g.n)
                w = P * (i + 1)
                for k0 in range(0, w, HALF):
                    n = min(HALF, w - k0)
                    mm = pe.matmul(max_ps[:, u % 2, k0:k0 + n], q_stack[g.slot][0:STACK, h, i * P:(i + 1) * P],
                                   k_stack[g.slot][0:STACK, k0:k0 + n], start=True, stop=True)
                mm.then_inc(scores_max, 1)

            def turn(g, after):
                pe.wait_ge(neg_done, SPLIT * (g.n + 1))
                if after is not None:
                    pe.wait_ge(max_read, UNITS * after.n + TURN - 1)
                pe.transpose(turn_ps, neg_max[:, :, :].rearrange("p m u -> p (m u)"), ident[:, :]).then_inc(turned, 1)

            def exp_scores(g, c, h):
                hf, j = CHUNKS[c]
                q0, w = start_of(c)
                i = c * GH + h
                if i == 0:
                    pe.wait_ge(neg_in, 16 * PARTS * (g.n + 1))
                wait(pe, exp_done, GH * NC * g.n + i - 1)
                mm = pe.matmul(exp_ps[:, i % 2, 0:w], k_stack[g.slot][0:STACKM, j * P:(j + 1) * P],
                               q_stack[g.slot][0:STACKM, h, q0:q0 + w], start=True, stop=c not in DIAG)
                if c in DIAG:
                    mm = pe.matmul(exp_ps[:, i % 2, 0:P], ident[:, :], future[:, :], start=False, stop=True)
                mm.then_inc(scores_exp, 1)

            def times_values(g, c):
                hf, j = CHUNKS[c]
                q0, w = start_of(c)
                pe.wait_ge(exp_done, GH * (NC * g.n + c + 1))
                if j == 0:
                    wait(pe, o_copied, 2 * g.n + hf - 1)
                o0 = q0 - hf * HALF
                for h in range(GH):
                    mm = pe.matmul(o_ps[h * 2 * HD:(h + 1) * 2 * HD, hf, o0:o0 + w], v_here[g.slot][:, j, :],
                                   probs[:, c % PRING, h, 0:w], start=(j == 0), stop=(j == (hf + 1) * ST // 2 - 1),
                                   skip_group_check=True)
                mm.then_inc(pv_done, 1)

            def step(g):
                for c in range(NC):
                    for h in range(GH):
                        exp_scores(g, c, h)
                        for kind, by, u in PLAN[c * GH + h]:
                            if kind == "u" and g.has(by):
                                max_scores(g.next(by), u)
                            if kind == "t" and g.has(by):
                                turn(g.next(by), g.next(by + 1) if g.has(by + 1) else None)
                    if c >= 2:
                        times_values(g, c - 2)
                    elif not (isinstance(g.n, int) and g.n == 0):
                        times_values(g.next(-1), NC + c - 2)

            pe.wait_ge(ones_set, SLOTS)
            pe.wait_ge(mask_set, 4)
            pe.wait_ge(ident_set, 2)
            for u in range(UNITS):
                max_scores(At(0, 0), u)
            for u in range(TURN):
                max_scores(At(0, 1), u)
            turn(At(0, 0), At(0, 1))
            for u in range(TURN, AHEAD):
                max_scores(At(0, 1), u)
            over_groups(pe, step)
            times_values(At(0, NG - 1), NC - 2)
            times_values(At(0, NG - 1), NC - 1)


def split_weights(act, dve, k, raw, hi, lo, hi_ready, lo_ready):
    if act is not None:
        act.activation(hi, raw, ACT.Copy).then_inc(hi_ready, 1)
    if dve is not None:
        dve.wait_ge(hi_ready, k + 1)
        dve.tensor_tensor(lo, raw, hi.bitcast(F32), ALU.subtract).then_inc(lo_ready, 1)


def phase_c(nc, x, wo_t, o_rows, x1, xn_t):
    with ExitStack() as ctx:
        def sb(name, shape, dt):
            return ctx.enter_context(nc.sbuf_tensor(name, shape, dt))

        def ps(name, shape):
            return ctx.enter_context(nc.psum_tensor(name, shape, F32))

        def sem(name):
            return ctx.enter_context(nc.semaphore(name))

        w_raw = sb("c_w_raw", [P, KT, HID], F32)
        w_hi = sb("c_w_hi", [P, KT, HID], F32R)
        w_lo = sb("c_w_lo", [P, KT, HID], F32R)
        ident = sb("c_ident", [P, P], F32)
        eps = sb("c_eps", [P, 1], F32)
        o_in = sb("c_o_in", [P, 2, NKV, P], F32)
        x_in = sb("c_x_in", [P, 2, HID], F32)
        rsum = sb("c_rsum", [P, 2, NH], F32)
        attn = sb("c_attn", [P, 2, HID], F32)
        attn_hi = sb("c_attn_hi", [P, 2, HID], F32R)
        attn_lo = sb("c_attn_lo", [P, 2, HID], F32R)
        x1_sb = sb("c_x1_sb", [P, 2, HID], F32)
        stats = sb("c_stats", [P, 2, 6], F32)
        mean_var = sb("c_mean_var", [P, 2, 2], F32)
        std = sb("c_std", [P, 2, 1], F32)
        rstd = sb("c_rstd", [P, 2, 1], F32)
        xn = sb("c_xn", [P, 2, HID], F32)
        xt_sb = sb("c_xt_sb", [P, 2, HID], F32)

        ot_ps = ps("c_ot_ps", [P, 2, 1024])
        at_ps = ps("c_at_ps", [P, HID])
        y_ps = ps("c_y_ps", [P, HID])
        xt_ps = ps("c_xt_ps", [P, HID])

        w_in = sem("c_w_in")
        o_loaded = [sem(f"c_o_loaded{s}") for s in range(2)]
        x_loaded = [sem(f"c_x_loaded{s}") for s in range(2)]
        x1_stored = [sem(f"c_x1_stored{s}") for s in range(2)]
        xt_stored = [sem(f"c_xt_stored{s}") for s in range(2)]
        pool_const = sem("c_pool_const")
        w_hi_ready = sem("c_w_hi_ready")
        w_lo_ready = sem("c_w_lo_ready")
        ot_done = sem("c_ot_done")
        rsum_done = sem("c_rsum_done")
        attn_done = sem("c_attn_done")
        at_done = sem("c_at_done")
        attn_hi_done = sem("c_attn_hi_done")
        attn_lo_done = sem("c_attn_lo_done")
        y_done = sem("c_y_done")
        x1_done = sem("c_x1_done")
        stats_done = sem("c_stats_done")
        var_done = sem("c_var_done")
        std_done = sem("c_std_done")
        rstd_done = sem("c_rstd_done")
        xn_done = sem("c_xn_done")
        xt_done = sem("c_xt_done")
        xt_copied = sem("c_xt_copied")
        passed = sem("c_passed")
        sp_passed = sem("c_sp_passed")

        block = ctx.enter_context(nc.Block())

        def tok(t):
            return bass.ds(t * P, P)

        def twice(s, t):
            return 16 * (t // 2 + 1) if isinstance(t, int) else 8 * (t - s) + 16

        @block.sync
        def _(sp):
            def load_o(t, s):
                wait(sp, ot_done, t - 1)
                if isinstance(t, int):
                    b, i = t // ST, t % ST
                    sp.dma_start(o_in[:, s, :, :], o_rows[b * NKV:(b + 1) * NKV, :, i * P:(i + 1) * P].rearrange("g p t -> p g t")
                                 ).then_inc(o_loaded[s], 16)
                else:
                    sp.dma_start(o_in[:, s, :, :], o_rows[bass.ds(t // ST * NKV, NKV), :, bass.ds(t % ST * P, P)].rearrange("g p t -> p g t")
                                 ).then_inc(o_loaded[s], 16)

            def load_x(t, s):
                wait(sp, x1_done, t - 1)
                sp.dma_start(x_in[:, s, :], x[tok(t), :]).then_inc(x_loaded[s], 16)

            def store(t, s):
                sp.wait_ge(x1_done, t + 1)
                sp.dma_start(x1[tok(t), :], x1_sb[:, s, :]).then_inc(x1_stored[s], 16)
                wait_apart(sp, xt_copied, t + 1, sp_passed)
                sp.dma_start(xn_t[:, tok(t)].rearrange("(k p) t -> p k t", p=P),
                             xt_sb[:, s, :].rearrange("p (k t) -> p k t", k=KT)).then_inc(xt_stored[s], 16)

            load_o(0, 0)
            load_o(1, 1)
            sp.dma_start(w_raw[:, :, :], wo_t.rearrange("(k p) n -> p k n", p=P)).then_inc(w_in, 16)
            load_x(0, 0)
            load_x(1, 1)
            load_o(2, 0)
            load_o(3, 1)
            with sp.Fori(2, TT // 2) as pair:
                for s in range(2):
                    t = 2 * pair + s
                    store(t - 4, s)
                    load_x(t - 2, s)
                    load_o(t, s)
            for t in range(TT - 2, TT):
                store(t - 2, t % 2)
                load_x(t, t % 2)
            for t in range(TT - 2, TT):
                store(t, t % 2)
            for s in range(2):
                sp.wait_ge(x1_stored[s], 8 * TT)
                sp.wait_ge(xt_stored[s], 8 * TT)

        @block.gpsimd
        def _(pool):
            identity(pool, pool_const, ident, 0)
            pool.memset(eps[:, :], EPS).then_inc(pool_const, 1)

        @block.scalar
        def _(act):
            act.wait_ge(pool_const, 3)

            def hi(t, s):
                act.wait_ge(at_done, t + 1)
                wait(act, y_done, t - 1)
                act.activation(attn_hi[:, s, :], at_ps[:, :], ACT.Copy).then_inc(attn_hi_done, 1)

            def std_of(t, s):
                act.wait_ge(var_done, t + 1)
                wait(act, rstd_done, t - 1)
                act.activation(std[:, s, :], mean_var[:, s, 1:2], ACT.Sqrt, bias=eps[:, :]).then_inc(std_done, 1)

            def out(t, s):
                act.wait_ge(xt_done, t + 1)
                if isinstance(t, int):
                    wait(act, xt_stored[s], 16 * (t // 2))
                else:
                    act.wait_ge(xt_stored[s], 8 * (t - s))
                act.activation(xt_sb[:, s, :], xt_ps[:, :], ACT.Copy).then_inc(xt_copied, 1)

            act.wait_ge(w_in, 16)
            for k in range(KT):
                split_weights(act, None, k, w_raw[:, k, :], w_hi[:, k, :], None, w_hi_ready, None)
            hi(0, 0)
            hi(1, 1)
            std_of(0, 0)
            hi(2, 0)
            std_of(1, 1)
            out(0, 0)
            with act.Fori(1, TT // 2 - 1) as pair:
                for s in range(2):
                    t = 2 * pair + s
                    hi(t + 1, 1 - s)
                    std_of(t, s)
                    out(t - 1, 1 - s)
            hi(TT - 1, 1)
            std_of(TT - 2, 0)
            out(TT - 3, 1)
            std_of(TT - 1, 1)
            out(TT - 2, 0)
            out(TT - 1, 1)

        @block.vector
        def _(dve):
            def divide(t, s):
                dve.wait_ge(ot_done, t + 1)
                wait(dve, at_done, t - 1)
                wait(dve, attn_done, t - 1)
                rows = ot_ps[:, s, :].rearrange("p (h r) -> p h r", r=2 * HD)
                dve.reciprocal(rsum[:, s, :].unsqueeze(2), rows[:, :, HD:HD + 1]).then_inc(rsum_done, 1)
                dve.wait_ge(rsum_done, t + 1)
                dve.tensor_tensor(attn[:, s, :].rearrange("p (h d) -> p h d", d=HD), rows[:, :, 0:HD],
                                  rsum[:, s, :].unsqueeze(2).to_broadcast([P, NH, HD]), ALU.mult).then_inc(attn_done, 1)

            def lo(t, s):
                dve.wait_ge(attn_hi_done, t + 1)
                dve.tensor_tensor(attn_lo[:, s, :], at_ps[:, :], attn_hi[:, s, :].bitcast(F32),
                                  ALU.subtract).then_inc(attn_lo_done, 1)

            def residual(t, s):
                dve.wait_ge(y_done, t + 1)
                dve.wait_ge(x_loaded[s], twice(s, t))
                if isinstance(t, int):
                    wait(dve, x1_stored[s], 16 * (t // 2))
                else:
                    dve.wait_ge(x1_stored[s], 8 * (t - s))
                wait(dve, xn_done, t - 1)
                dve.tensor_tensor(x1_sb[:, s, :], y_ps[:, :], x_in[:, s, :], ALU.add).then_inc(x1_done, 1)
                dve.wait_ge(x1_done, t + 1)
                wait(dve, std_done, t - 1)
                dve.bn_stats(stats[:, s, :], x1_sb[:, s, :]).then_inc(stats_done, 1)
                wait_apart(dve, stats_done, t + 1, passed)
                dve.bn_aggr(mean_var[:, s, :], stats[:, s, :]).then_inc(var_done, 1)

            def normalise(t, s):
                dve.wait_ge(std_done, t + 1)
                dve.reciprocal(rstd[:, s, :], std[:, s, :]).then_inc(rstd_done, 1)
                dve.wait_ge(rstd_done, t + 1)
                wait(dve, xt_done, t - 1)
                dve.tensor_scalar(xn[:, s, :], x1_sb[:, s, :], mean_var[:, s, 0:1], rstd[:, s, :],
                                  ALU.subtract, ALU.mult).then_inc(xn_done, 1)

            divide(0, 0)
            for k in range(KT):
                split_weights(None, dve, k, w_raw[:, k, :], w_hi[:, k, :], w_lo[:, k, :], w_hi_ready, w_lo_ready)
            divide(1, 1)
            lo(0, 0)
            divide(2, 0)
            lo(1, 1)
            residual(0, 0)
            normalise(0, 0)
            divide(3, 1)
            lo(2, 0)
            residual(1, 1)
            normalise(1, 1)
            with dve.Fori(1, TT // 2 - 1) as pair:
                for s in range(2):
                    t = 2 * pair + s
                    divide(t + 2, s)
                    lo(t + 1, 1 - s)
                    residual(t, s)
                    normalise(t, s)
            lo(TT - 1, 1)
            for t in range(TT - 2, TT):
                residual(t, t % 2)
                normalise(t, t % 2)

        @block.tensor
        def _(pe):
            def o_transposes(t, s):
                pe.wait_ge(o_loaded[s], twice(s, t))
                wait(pe, attn_done, t - 1)
                for g in range(NKV):
                    mm = pe.transpose(ot_ps[:, s, g * P:(g + 1) * P], o_in[:, s, g, :], ident[:, :])
                mm.then_inc(ot_done, 1)

            def a_transposes(t, s):
                pe.wait_ge(attn_done, t + 1)
                wait(pe, attn_lo_done, t)
                for k in range(KT):
                    mm = pe.transpose(at_ps[:, k * P:(k + 1) * P], attn[:, s, k * P:(k + 1) * P], ident[:, :])
                mm.then_inc(at_done, 1)

            def products(t, s):
                pe.wait_ge(attn_lo_done, t + 1)
                wait(pe, x1_done, t)
                n = 0
                for k in range(KT):
                    for a, w in ((attn_hi, w_hi), (attn_hi, w_lo), (attn_lo, w_hi)):
                        mm = pe.matmul(y_ps[:, :], a[:, s, k * P:(k + 1) * P], w[:, k, :],
                                       start=(n == 0), stop=(n == 3 * KT - 1))
                        n += 1
                mm.then_inc(y_done, 1)

            def x_transposes(t, s):
                pe.wait_ge(xn_done, t + 1)
                wait(pe, xt_copied, t)
                for k in range(KT):
                    mm = pe.transpose(xt_ps[:, k * P:(k + 1) * P], xn[:, s, k * P:(k + 1) * P], ident[:, :])
                mm.then_inc(xt_done, 1)

            pe.wait_ge(pool_const, 2)
            o_transposes(0, 0)
            o_transposes(1, 1)
            a_transposes(0, 0)
            o_transposes(2, 0)
            a_transposes(1, 1)
            pe.wait_ge(w_lo_ready, KT)
            products(0, 0)
            o_transposes(3, 1)
            a_transposes(2, 0)
            products(1, 1)
            x_transposes(0, 0)
            with pe.Fori(1, TT // 2 - 1) as pair:
                for s in range(2):
                    t = 2 * pair + s
                    o_transposes(t + 2, s)
                    a_transposes(t + 1, 1 - s)
                    products(t, s)
                    x_transposes(t - 1, 1 - s)
            a_transposes(TT - 1, 1)
            products(TT - 2, 0)
            x_transposes(TT - 3, 1)
            products(TT - 1, 1)
            x_transposes(TT - 2, 0)
            x_transposes(TT - 1, 1)


def phase_d(nc, wg_t, wu_t, wd_t, x1, xn_t, out):
    CT = 4
    CW = CT * P
    NCH = TT // CT

    def rows(i):
        return min(P, INTER - i * P)

    with ExitStack() as ctx:
        def sb(name, shape, dt):
            return ctx.enter_context(nc.sbuf_tensor(name, shape, dt))

        def ps(name, shape):
            return ctx.enter_context(nc.psum_tensor(name, shape, F32))

        def sem(name):
            return ctx.enter_context(nc.semaphore(name))

        w_raw = sb("d_w_raw", [P, 2, INTER], F32)
        wg = [sb(f"d_wg_{n}", [P, KT, INTER], F32R) for n in ("hi", "lo")]
        wu = [sb(f"d_wu_{n}", [P, KT, INTER], F32R) for n in ("hi", "lo")]
        wd = [sb(f"d_wd_{n}", [P, IT, HID], F32R) for n in ("hi", "lo")]
        xn = sb("d_xn", [P, 1, KT, CW], F32)
        xn_hi = sb("d_xn_hi", [P, KT, CW], F32R)
        xn_lo = sb("d_xn_lo", [P, KT, CW], F32R)
        x1_in = sb("d_x1_in", [P, CT, HID], F32)
        gate = sb("d_gate", [P, 2, CW], F32)
        prod = sb("d_prod", [P, 1, CW], F32)
        h_hi = sb("d_h_hi", [P, 2, CW], F32R)
        h_lo = sb("d_h_lo", [P, 2, CW], F32R)
        out_sb = sb("d_out_sb", [P, 2, HID], F32)

        g_ps = ps("d_g_ps", [P, 2, CW])
        u_ps = ps("d_u_ps", [P, 2, CW])
        y_ps = ps("d_y_ps", [P, CT, HID])

        w_loaded = [sem(f"d_w_loaded{s}") for s in range(2)]
        w_hi_ready = sem("d_w_hi_ready")
        w_lo_ready = sem("d_w_lo_ready")
        xn_in = sem("d_xn_in")
        x1_loaded = sem("d_x1_loaded")
        xn_hi_done = sem("d_xn_hi_done")
        xn_lo_done = sem("d_xn_lo_done")
        g_done = sem("d_g_done")
        u_done = sem("d_u_done")
        gate_done = sem("d_gate_done")
        prod_done = sem("d_prod_done")
        h_hi_done = sem("d_h_hi_done")
        h_lo_done = sem("d_h_lo_done")
        y_step = sem("d_y_step")
        out_done = sem("d_out_done")
        out_stored = [sem(f"d_out_stored{s}") for s in range(2)]

        steps = []
        for k in range(KT):
            for w_dram, w in ((wg_t, wg), (wu_t, wu)):
                steps.append((w_dram[k * P:(k + 1) * P, :], P, INTER, w[0][:, k, :], w[1][:, k, :]))
        for i in range(0, IT - 1, 2):
            steps.append((wd_t[i * P:(i + 2) * P, :].rearrange("(a p) n -> p a n", p=P), P, 2 * HID,
                          wd[0][:, i:i + 2, :].rearrange("p a n -> p (a n)"), wd[1][:, i:i + 2, :].rearrange("p a n -> p (a n)")))
        r = rows(IT - 1)
        steps.append((wd_t[(IT - 1) * P:INTER, :], r, HID, wd[0][0:r, IT - 1, :], wd[1][0:r, IT - 1, :]))
        W_GU = 2 * KT

        block = ctx.enter_context(nc.Block())

        @block.sync
        def _(sp):
            def load_w(k):
                src, r, n, _, _ = steps[k]
                wait(sp, w_lo_ready, k - 1)
                dst = w_raw[0:r, k % 2, 0:n]
                if len(src.shape) == 3:
                    dst = dst.rearrange("p (a n) -> p a n", a=2)
                sp.dma_start(dst, src).then_inc(w_loaded[k % 2], 16)

            def load_xn(c):
                wait(sp, xn_lo_done, KT * c)
                sp.dma_start(xn[:, 0, :, :], xn_t[:, bass.ds(c * CW, CW)].rearrange("(k p) t -> p k t", p=P)).then_inc(xn_in, 16)

            def load_x1(c):
                wait(sp, out_done, CT * c)
                sp.dma_start(x1_in[:, :, :], x1[bass.ds(c * CW, CW), :].rearrange("(a p) n -> p a n", p=P)).then_inc(x1_loaded, 16)

            def store(c):
                for a in range(CT):
                    sp.wait_ge(out_done, CT * c + a + 1)
                    sp.dma_start(out[bass.ds(c * CW + a * P, P), :], out_sb[:, a % 2, :]).then_inc(out_stored[a % 2], 16)

            load_w(0)
            load_w(1)
            load_xn(0)
            for k in range(2, len(steps)):
                load_w(k)
            load_x1(0)
            load_xn(1)
            with sp.Fori(0, NCH - 2) as c:
                store(c)
                load_x1(c + 1)
                load_xn(c + 2)
            store(NCH - 2)
            load_x1(NCH - 1)
            store(NCH - 1)
            sp.wait_ge(out_stored[0], 16 * NCH * CT // 2)
            sp.wait_ge(out_stored[1], 16 * NCH * CT // 2)

        @block.scalar
        def _(act):
            def weight(k):
                src, r, n, hi, _ = steps[k]
                act.wait_ge(w_loaded[k % 2], 16 * (k // 2 + 1))
                act.activation(hi, w_raw[0:r, k % 2, 0:n], ACT.Copy).then_inc(w_hi_ready, 1)

            def split_xn(c):
                act.wait_ge(xn_in, 16 * (c + 1))
                wait(act, u_done, IT * c)
                for k in range(KT):
                    act.activation(xn_hi[:, k, :], xn[:, 0, k, :], ACT.Copy).then_inc(xn_hi_done, 1)

            def silu(c, i):
                n = IT * c + i
                r = rows(i)
                act.wait_ge(g_done, n + 1)
                wait(act, prod_done, n - 1)
                act.activation(gate[0:r, i % 2, :], g_ps[0:r, i % 2, :], ACT.Silu).then_inc(gate_done, 1)

            def hi(c, i):
                n = IT * c + i
                r = rows(i)
                act.wait_ge(prod_done, n + 1)
                wait(act, y_step, n - 1)
                act.activation(h_hi[0:r, i % 2, :], prod[0:r, 0, :], ACT.Copy).then_inc(h_hi_done, 1)

            for k in range(W_GU):
                weight(k)
            split_xn(0)
            for k in range(W_GU, len(steps)):
                weight(k)

            def chunk(c):
                for i in range(IT):
                    silu(c, i)
                    if i >= 1:
                        hi(c, i - 1)
                hi(c, IT - 1)

            chunk(0)
            with act.Fori(1, NCH) as c:
                split_xn(c)
                chunk(c)

        @block.vector
        def _(dve):
            def weight(k):
                src, r, n, hi, lo = steps[k]
                split_weights(None, dve, k, w_raw[0:r, k % 2, 0:n], hi, lo, w_hi_ready, w_lo_ready)

            def split_xn(c):
                for k in range(KT):
                    dve.wait_ge(xn_hi_done, KT * c + k + 1)
                    dve.tensor_tensor(xn_lo[:, k, :], xn[:, 0, k, :], xn_hi[:, k, :].bitcast(F32),
                                      ALU.subtract).then_inc(xn_lo_done, 1)

            def product(c, i):
                n = IT * c + i
                r = rows(i)
                dve.wait_ge(gate_done, n + 1)
                dve.wait_ge(u_done, n + 1)
                wait(dve, h_lo_done, n)
                dve.tensor_tensor(prod[0:r, 0, :], u_ps[0:r, i % 2, :], gate[0:r, i % 2, :], ALU.mult).then_inc(prod_done, 1)

            def lo(c, i):
                n = IT * c + i
                r = rows(i)
                dve.wait_ge(h_hi_done, n + 1)
                dve.tensor_tensor(h_lo[0:r, i % 2, :], prod[0:r, 0, :], h_hi[0:r, i % 2, :].bitcast(F32),
                                  ALU.subtract).then_inc(h_lo_done, 1)

            def add(c):
                dve.wait_ge(x1_loaded, 16 * (c + 1))
                dve.wait_ge(y_step, IT * (c + 1))
                for a in range(CT):
                    if isinstance(c, int):
                        wait(dve, out_stored[a % 2], 16 * (c * CT // 2 + a // 2))
                    else:
                        dve.wait_ge(out_stored[a % 2], 16 * (c * (CT // 2) + a // 2))
                    dve.tensor_tensor(out_sb[:, a % 2, :], y_ps[:, a, :], x1_in[:, a, :], ALU.add).then_inc(out_done, 1)

            for k in range(W_GU):
                weight(k)
            split_xn(0)
            for k in range(W_GU, len(steps)):
                weight(k)

            def chunk(c):
                for i in range(IT):
                    product(c, i)
                    lo(c, i)

            chunk(0)
            add(0)
            with dve.Fori(1, NCH) as c:
                split_xn(c)
                chunk(c)
                add(c)

        @block.tensor
        def _(pe):
            def up(c, i, w, bank, done):
                r = rows(i)
                n = 0
                for k in range(KT):
                    cols = slice(i * P, i * P + r)
                    for a, b in ((w[0], xn_hi), (w[0], xn_lo), (w[1], xn_hi)):
                        mm = pe.matmul(bank[0:r, i % 2, :], a[:, k, cols], b[:, k, :], start=(n == 0), stop=(n == 3 * KT - 1))
                        n += 1
                mm.then_inc(done, 1)

            def down(c, i):
                r = rows(i)
                pe.wait_ge(h_lo_done, IT * c + i + 1)
                if i == 0:
                    wait(pe, out_done, CT * c)
                for a in range(CT):
                    toks = slice(a * P, (a + 1) * P)
                    for n, (h, w) in enumerate(((h_hi, wd[0]), (h_hi, wd[1]), (h_lo, wd[0]))):
                        mm = pe.matmul(y_ps[:, a, :], h[0:r, i % 2, toks], w[0:r, i, :],
                                       start=(i == 0 and n == 0), stop=(i == IT - 1 and n == 2))
                mm.then_inc(y_step, 1)

            def chunk(c, first=False):
                pe.wait_ge(xn_lo_done, KT * (c + 1))
                for i in range(IT):
                    n = IT * c + i
                    wait(pe, prod_done, n - 1)
                    up(c, i, wg, g_ps, g_done)
                    up(c, i, wu, u_ps, u_done)
                    if i >= 1:
                        if first and i == 1:
                            pe.wait_ge(w_lo_ready, len(steps))
                        down(c, i - 1)
                down(c, IT - 1)

            pe.wait_ge(w_lo_ready, W_GU)
            chunk(0, True)
            with pe.Fori(1, NCH) as c:
                chunk(c)


def transformer_layer(nc, x, wqkv_t, wo_t, wg_t, wu_t, wd_t, cos_t, sin_t, out):
    q_parts = nc.dram_tensor("q_parts", [PARTS, BATCH * QROWS, SEQ], BF16, kind="Internal").ap()
    k_parts = nc.dram_tensor("k_parts", [PARTS, BATCH * KROWS, SEQ], BF16, kind="Internal").ap()
    o_rows = nc.dram_tensor("o_rows", [NG, P, SEQ], F32, kind="Internal").ap()
    x1 = nc.dram_tensor("x1", [TOK, HID], F32, kind="Internal").ap()
    xn_t = nc.dram_tensor("xn_t", [HID, TOK], F32, kind="Internal").ap()
    with nc.sbuf_tensor("v_all", [P, NG, ST, 2 * HD], F32) as v_all:
        phase_a(nc, x, wqkv_t, cos_t, sin_t, q_parts, k_parts, v_all)
        phase_b(nc, q_parts, k_parts, v_all, o_rows)
    phase_c(nc, x, wo_t, o_rows, x1, xn_t)
    phase_d(nc, wg_t, wu_t, wd_t, x1, xn_t, out)


def kernel(L0_attn_hidden_states, L0_attn_Wq, L0_attn_Wk, L0_attn_Wv, L0_attn_Wo, L0_ffn_w_gate, L0_ffn_w_up,
           L0_ffn_w_down):
    import numpy as np
    import concourse.bacc as bacc
    from concourse.bass_utils import run_bass_kernel_spmd

    inv_freq = (1.0 / np.float32(10000.0) ** (np.arange(0, HD, 2, dtype=np.float32) / np.float32(HD))).astype(np.float32)
    angle = np.outer(np.arange(SEQ, dtype=np.float32), inv_freq).astype(np.float32)
    cos_t = np.concatenate([np.cos(angle), np.cos(angle)], axis=1).astype(np.float32)
    sin_t = np.concatenate([-np.sin(angle), np.sin(angle)], axis=1).astype(np.float32)

    def turned(w):
        return np.ascontiguousarray(np.asarray(w).T)

    arrays = {
        "x": np.ascontiguousarray(np.asarray(L0_attn_hidden_states).reshape(TOK, HID)),
        "wqkv_t": turned(np.concatenate([np.asarray(L0_attn_Wq), np.asarray(L0_attn_Wk), np.asarray(L0_attn_Wv)], axis=0)),
        "wo_t": turned(L0_attn_Wo),
        "wg_t": turned(L0_ffn_w_gate),
        "wu_t": turned(L0_ffn_w_up),
        "wd_t": turned(L0_ffn_w_down),
        "cos_t": cos_t,
        "sin_t": sin_t,
    }
    nc = bacc.Bacc("TRN2", target_bir_lowering=False, num_devices=1)
    args = [nc.dram_tensor(f"in_{name}", a.shape, mybir.dt.from_np(a.dtype), kind="ExternalInput").ap()
            for name, a in arrays.items()]
    out = nc.dram_tensor("out_0", (TOK, HID), F32, kind="ExternalOutput").ap()
    transformer_layer(nc, *args, out)
    r = run_bass_kernel_spmd(nc, [{f"in_{name}": a for name, a in arrays.items()}], core_ids=[0])
    return r.results[0]["out_0"].reshape(BATCH, SEQ, HID)
```

```python
from contextlib import ExitStack

import concourse.bass as bass
from concourse import mybir

ALU = mybir.AluOpType
ACT = mybir.ActivationFunctionType
F32 = mybir.dt.float32
F32R = mybir.dt.float32r
BF16 = mybir.dt.bfloat16

P = 128
HID = 512
KT = HID // P
BATCH, SEQ = 2, 1024
TOK = BATCH * SEQ
TT = TOK // P
ST = SEQ // P
NH, NKV = 32, 8
HD = HID // NH
GH = NH // NKV
QROWS, KROWS = NH * HD, NKV * HD
QK = QROWS + KROWS
QKV = QK + KROWS
QKT = QK // P
NG = BATCH * NKV
PARTS = 3
STACK = 6 * HD
STACKM = STACK + PARTS
INTER = 1376
IT = -(-INTER // P)
EPS = 1e-5
SCALE = HD ** -0.5
NEG = -3.0e38


def wait(engine, sem, value):
    if not (isinstance(value, int) and value <= 0):
        engine.wait_ge(sem, value)


def wait_apart(engine, sem, value, passed):
    if not (isinstance(value, int) and value <= 0):
        engine.wait_ge(sem, value)
        if not isinstance(value, int):
            engine.sem_inc(passed, 1)


def identity(engine, sem, tensor, n):
    engine.memset(tensor[:, :], 0.0).then_inc(sem, 1)
    engine.wait_ge(sem, n + 1)
    engine.affine_select(out=tensor[:, :], in_=tensor[:, :], compare_op=ALU.not_equal, fill=1.0, base=0,
                         pattern=[[-1, P]], channel_multiplier=1).then_inc(sem, 1)


def over_tiles(engine, step):
    for t in range(-2, 4):
        step(t, t % 2)
    with engine.Fori(2, TT // 2 - 1) as pair:
        step(2 * pair, 0)
        step(2 * pair + 1, 1)
    for t in range(TT - 2, TT + 2):
        step(t, t % 2)


def exists(t):
    return not isinstance(t, int) or 0 <= t < TT


def earlier(t, s):
    return t // 2 if isinstance(t, int) else (t - s) // 2


def phase_a(nc, x, wqkv_t, cos_t, sin_t, q_parts, k_parts, v_all):
    with ExitStack() as ctx:
        def sb(name, shape, dt):
            return ctx.enter_context(nc.sbuf_tensor(name, shape, dt))

        def ps(name, shape):
            return ctx.enter_context(nc.psum_tensor(name, shape, F32))

        def sem(name):
            return ctx.enter_context(nc.semaphore(name))

        w_raw = sb("a_w_raw", [P, KT, QKV], F32)
        w_hi = sb("a_w_hi", [P, KT, QKV], F32R)
        w_lo = sb("a_w_lo", [P, KT, QKV], F32R)
        cos = sb("a_cos", [P, TT, HD], F32)
        sin = sb("a_sin", [P, TT, HD], F32)
        ident = sb("a_ident", [P, P], F32)
        x_in = sb("a_x_in", [P, 2, HID], F32)
        stats = sb("a_stats", [P, 2, 6], F32)
        mean_var = sb("a_mean_var", [P, 2, 2], F32)
        std = sb("a_std", [P, 2, 1], F32)
        rstd = sb("a_rstd", [P, 2, 1], F32)
        eps = sb("a_eps", [P, 1], F32)
        xn = sb("a_xn", [P, 2, HID], F32)
        xn_hi = sb("a_xn_hi", [P, 2, HID], F32R)
        xn_lo = sb("a_xn_lo", [P, 2, HID], F32R)
        by_cos = sb("a_by_cos", [P, 2, QK], F32)
        by_sin = sb("a_by_sin", [P, 2, QK], F32)
        roped = sb("a_roped", [P, 2, QK], F32)
        rest = sb("a_rest", [P, 2, QK], F32)
        parts = sb("a_parts", [P, PARTS, QKT, TOK], BF16)

        xt_ps = ps("a_xt_ps", [P, 2, HID])
        qkv_ps = ps("a_qkv_ps", [P, 2, 1024])
        rt_ps = ps("a_rt_ps", [P, 1024])

        weights_in = sem("a_weights_in")
        tables_in = sem("a_tables_in")
        x_loaded = [sem(f"a_x_loaded{s}") for s in range(2)]
        parts_out = sem("a_parts_out")
        pool_const = sem("a_pool_const")
        ones_set = sem("a_ones_set")
        w_hi_ready = sem("a_w_hi_ready")
        w_lo_ready = sem("a_w_lo_ready")
        stats_done = sem("a_stats_done")
        var_done = sem("a_var_done")
        std_done = sem("a_std_done")
        rstd_done = sem("a_rstd_done")
        xn_done = sem("a_xn_done")
        xt_done = sem("a_xt_done")
        xn_hi_done = sem("a_xn_hi_done")
        passed = sem("a_passed")
        xn_lo_done = sem("a_xn_lo_done")
        qkv_done = sem("a_qkv_done")
        cos_done = sem("a_cos_done")
        sin_done = sem("a_sin_done")
        v_done = sem("a_v_done")
        roped_done = sem("a_roped_done")
        rt_done = sem("a_rt_done")
        part0_done = sem("a_part0_done")
        rest_done = sem("a_rest_done")
        part1_done = sem("a_part1_done")
        part2_done = sem("a_part2_done")

        block = ctx.enter_context(nc.Block())

        def tok(t):
            return bass.ds(t * P, P)

        def store(engine, b):
            for done in (part0_done, part1_done, part2_done):
                engine.wait_ge(done, ST * (b + 1))
            for m in range(PARTS):
                at = bass.ds(b * SEQ, SEQ)
                engine.dma_start(q_parts[m, b * QROWS:(b + 1) * QROWS, :].rearrange("(c p) t -> p c t", p=P),
                                 parts[:, m, 0:QROWS // P, at]).then_inc(parts_out, 16)
                engine.dma_start(k_parts[m, b * KROWS:(b + 1) * KROWS, :],
                                 parts[:, m, QROWS // P, at]).then_inc(parts_out, 16)

        @block.sync
        def _(sp):
            sp.dma_start(x_in[:, 0, :], x[0:P, :]).then_inc(x_loaded[0], 16)
            sp.dma_start(x_in[:, 1, :], x[P:2 * P, :]).then_inc(x_loaded[1], 16)
            sp.dma_start(w_raw[:, :, :], wqkv_t.rearrange("(k p) n -> p k n", p=P)).then_inc(weights_in, 16)
            for b in range(BATCH):
                sp.dma_start(cos[:, b * ST:(b + 1) * ST, :], cos_t.rearrange("(t p) d -> p t d", p=P)).then_inc(tables_in, 16)
                sp.dma_start(sin[:, b * ST:(b + 1) * ST, :], sin_t.rearrange("(t p) d -> p t d", p=P)).then_inc(tables_in, 16)

            def load(t, s):
                sp.wait_ge(xn_done, t - 1)
                sp.dma_start(x_in[:, s, :], x[tok(t), :]).then_inc(x_loaded[s], 16)

            with sp.Fori(1, TT // 2) as pair:
                load(2 * pair, 0)
                load(2 * pair + 1, 1)
            store(sp, 1)
            sp.wait_ge(parts_out, 16 * 2 * PARTS * BATCH)

        @block.gpsimd
        def _(pool):
            identity(pool, pool_const, ident, 0)
            pool.memset(eps[:, :], EPS).then_inc(pool_const, 1)
            pool.memset(v_all[:, :, :, :], 1.0).then_inc(ones_set, 1)

            def add(t, s):
                pool.wait_ge(cos_done, t + 1)
                pool.wait_ge(sin_done, 2 * t + 2)
                wait(pool, rt_done, t - 1)
                pool.tensor_tensor(roped[:, s, :], by_cos[:, s, :], by_sin[:, s, :], ALU.add).then_inc(roped_done, 1)

            def last_part(t, s):
                pool.wait_ge(part1_done, t + 1)
                pool.tensor_tensor(parts[:, 2, :, tok(t)], rest[:, s, :].rearrange("p (c t) -> p c t", c=QKT),
                                   parts[:, 1, :, tok(t)], ALU.subtract).then_inc(part2_done, 1)

            def step(t, s):
                if exists(t - 2):
                    last_part(t - 2, s)
                if exists(t):
                    add(t, s)

            over_tiles(pool, step)

        @block.scalar
        def _(act):
            def std_of(t, s):
                act.wait_ge(var_done, t + 1)
                wait(act, rstd_done, t - 1)
                act.activation(std[:, s, :], mean_var[:, s, 1:2], ACT.Sqrt, bias=eps[:, :]).then_inc(std_done, 1)

            def hi(t, s):
                act.wait_ge(xt_done, t + 1)
                wait(act, qkv_done, t - 1)
                act.activation(xn_hi[:, s, :], xt_ps[:, s, :], ACT.Copy).then_inc(xn_hi_done, 1)

            def values(t, s):
                act.wait_ge(sin_done, 2 * t + 2)
                src = qkv_ps[:, s, QK:QKV].rearrange("p (g d) -> p g d", d=HD)
                act.activation(v_all[:, bass.ds(group_row(t), NKV), tile_of(t), 0:HD], src, ACT.Copy).then_inc(v_done, 1)

            def group_row(t):
                return (t // ST) * NKV

            def tile_of(t):
                return t % ST

            def first_parts(t, s):
                act.wait_ge(rt_done, t + 1)
                act.activation(parts[:, 0, :, tok(t)], rt_ps[:, 0:QK].rearrange("p (c t) -> p c t", c=QKT),
                               ACT.Copy).then_inc(part0_done, 1)

            def second_part(t, s):
                act.wait_ge(rest_done, t + 1)
                act.activation(parts[:, 1, :, tok(t)], rest[:, s, :].rearrange("p (c t) -> p c t", c=QKT),
                               ACT.Copy).then_inc(part1_done, 1)

            def step(t, s):
                if exists(t + 1):
                    hi(t + 1, 1 - s)
                if exists(t + 2):
                    std_of(t + 2, s)
                if isinstance(t, int) and t == -2:
                    act.wait_ge(weights_in, 16)
                    for k in range(KT):
                        act.activation(w_hi[:, k, :], w_raw[:, k, :], ACT.Copy).then_inc(w_hi_ready, 1)
                if exists(t - 2):
                    first_parts(t - 2, s)
                    second_part(t - 2, s)
                if exists(t):
                    values(t, s)
                if isinstance(t, int) and t == TT - 2:
                    store(act, 0)

            act.wait_ge(pool_const, 3)
            act.wait_ge(ones_set, 1)
            over_tiles(act, step)

        @block.vector
        def _(dve):
            def moments(t, s):
                if isinstance(t, int):
                    dve.wait_ge(x_loaded[s], 16 * (t // 2 + 1))
                else:
                    dve.wait_ge(x_loaded[s], 8 * (t - s) + 16)
                wait(dve, std_done, t - 1)
                wait(dve, xn_done, t - 1)
                dve.bn_stats(stats[:, s, :], x_in[:, s, :]).then_inc(stats_done, 1)
                wait_apart(dve, stats_done, t + 1, passed)
                dve.bn_aggr(mean_var[:, s, :], stats[:, s, :]).then_inc(var_done, 1)

            def normalise(t, s):
                dve.wait_ge(std_done, t + 1)
                dve.reciprocal(rstd[:, s, :], std[:, s, :]).then_inc(rstd_done, 1)
                dve.wait_ge(rstd_done, t + 1)
                wait(dve, xt_done, t - 1)
                dve.tensor_scalar(xn[:, s, :], x_in[:, s, :], mean_var[:, s, 0:1], rstd[:, s, :],
                                  ALU.subtract, ALU.mult).then_inc(xn_done, 1)

            def lo(t, s):
                dve.wait_ge(xn_hi_done, t + 1)
                dve.tensor_tensor(xn_lo[:, s, :], xt_ps[:, s, :], xn_hi[:, s, :].bitcast(F32),
                                  ALU.subtract).then_inc(xn_lo_done, 1)

            def rotate(t, s):
                dve.wait_ge(qkv_done, t + 1)
                wait(dve, roped_done, t - 1)
                heads = qkv_ps[:, s, 0:QK].rearrange("p (h d) -> p h d", d=HD)
                n = NH + NKV
                dve.tensor_tensor(by_cos[:, s, :].rearrange("p (h d) -> p h d", d=HD), heads,
                                  cos[:, bass.ds(t, 1), :].to_broadcast([P, n, HD]),
                                  ALU.mult).then_inc(cos_done, 1)
                to = by_sin[:, s, :].rearrange("p (h d) -> p h d", d=HD)
                half = HD // 2
                for a, b in ((0, half), (half, 0)):
                    dve.tensor_tensor(to[:, :, a:a + half], heads[:, :, b:b + half],
                                      sin[:, bass.ds(t, 1), a:a + half].to_broadcast([P, n, half]),
                                      ALU.mult).then_inc(sin_done, 1)

            def remainder(t, s):
                dve.wait_ge(part0_done, t + 1)
                wait(dve, part2_done, t - 1)
                wait(dve, part1_done, t - 1)
                dve.tensor_tensor(rest[:, s, :].rearrange("p (c t) -> p c t", c=QKT),
                                  rt_ps[:, 0:QK].rearrange("p (c t) -> p c t", c=QKT),
                                  parts[:, 0, :, tok(t)], ALU.subtract).then_inc(rest_done, 1)

            def step(t, s):
                if exists(t + 1):
                    lo(t + 1, 1 - s)
                if exists(t + 2):
                    moments(t + 2, s)
                    normalise(t + 2, s)
                if isinstance(t, int) and t == -2:
                    for k in range(KT):
                        dve.wait_ge(w_hi_ready, k + 1)
                        dve.tensor_tensor(w_lo[:, k, :], w_raw[:, k, :], w_hi[:, k, :].bitcast(F32),
                                          ALU.subtract).then_inc(w_lo_ready, 1)
                    dve.wait_ge(tables_in, 64)
                if exists(t - 2):
                    remainder(t - 2, s)
                if exists(t):
                    rotate(t, s)

            over_tiles(dve, step)

        @block.tensor
        def _(pe):
            def x_transposes(t, s):
                pe.wait_ge(xn_done, t + 1)
                wait(pe, xn_lo_done, t - 1)
                for k in range(KT):
                    mm = pe.transpose(xt_ps[:, s, k * P:(k + 1) * P], xn[:, s, k * P:(k + 1) * P], ident[:, :])
                mm.then_inc(xt_done, 1)

            def products(t, s):
                pe.wait_ge(xn_hi_done, t + 1)
                pe.wait_ge(xn_lo_done, t + 1)
                wait(pe, v_done, t - 1)
                wait(pe, cos_done, t - 1)
                wait(pe, sin_done, 2 * t - 2)
                for c0, c1 in ((0, QROWS), (QROWS, QKV)):
                    n = 0
                    for k in range(KT):
                        for a, w in ((xn_hi, w_hi), (xn_hi, w_lo), (xn_lo, w_hi)):
                            mm = pe.matmul(qkv_ps[:, s, c0:c1], a[:, s, k * P:(k + 1) * P], w[:, k, c0:c1],
                                           start=(n == 0), stop=(n == 3 * KT - 1))
                            n += 1
                mm.then_inc(qkv_done, 1)

            def r_transposes(t, s):
                pe.wait_ge(roped_done, t + 1)
                wait(pe, rest_done, t)
                for c in range(QKT):
                    mm = pe.transpose(rt_ps[:, c * P:(c + 1) * P], roped[:, s, c * P:(c + 1) * P], ident[:, :])
                mm.then_inc(rt_done, 1)

            def step(t, s):
                if exists(t + 1):
                    x_transposes(t + 1, 1 - s)
                if exists(t - 2):
                    r_transposes(t - 2, s)
                if exists(t):
                    if isinstance(t, int) and t == 0:
                        pe.wait_ge(w_lo_ready, KT)
                    products(t, s)

            pe.wait_ge(pool_const, 2)
            over_tiles(pe, step)


def phase_b(nc, q_parts, k_parts, v_all, o_rows):
    UNITS = GH * ST
    AHEAD = 6
    TURN = 2
    SLOTS = 3
    HALF = SEQ // 2
    CHUNKS = [(hf, j) for hf in range(2) for j in range((hf + 1) * ST // 2)]
    NC = len(CHUNKS)
    DIAG = [c for c, (hf, j) in enumerate(CHUNKS) if j * P >= hf * HALF]
    PRING = 4
    ERING = 3

    class At:
        def __init__(self, p, k):
            self.p, self.k = p, k
            self.n, self.slot, self.turn = SLOTS * p + k, k % SLOTS, p + k // SLOTS

        def next(self, by=1):
            return At(self.p, self.k + by)

        def has(self, by=1):
            return not isinstance(self.n, int) or self.n + by < NG

    def start_of(c):
        hf, j = CHUNKS[c]
        q0 = max(hf * HALF, j * P)
        return q0, (hf + 1) * HALF - q0

    def unit_of(u):
        return ST - 1 - u // GH, u % GH

    def banks_of(u):
        wide = unit_of(u)[0] >= ST // 2
        return (2 * (u % 2), 2) if wide else (u % 4, 1)

    def room_at(u):
        b0, nb = banks_of(u)
        for v in range(u - 1, u - UNITS, -1):
            c0, ncb = banks_of(v % UNITS)
            if b0 < c0 + ncb and c0 < b0 + nb:
                return v + 1

    def plan():
        events = [("u", 1, u) for u in range(AHEAD, UNITS)]
        events += [("u", 2, u) for u in range(TURN)] + [("t", 1, 0)] + [("u", 2, u) for u in range(TURN, AHEAD)]
        cost = [P * (unit_of(u)[0] + 1) + 60 if kind == "u" else P for kind, _, u in events]
        work = [start_of(c)[1] for c in range(NC) for _ in range(GH)]
        out, e, done, made = [], 0, 0, 0
        for wk in work:
            made += wk
            here = []
            while e < len(events) and (done + cost[e] / 2) * sum(work) <= made * sum(cost):
                here.append(events[e])
                done += cost[e]
                e += 1
            out.append(here)
        out[-1] += events[e:]
        return out

    PLAN = plan()
    TURN_AT = next(i for i, here in enumerate(PLAN) if ("t", 1, 0) in here)

    def over_groups(engine, step):
        step(At(0, 0))
        with engine.Fori(0, (NG - 4) // SLOTS) as p:
            for k in range(1, SLOTS + 1):
                step(At(p, k))
        for n in range(NG - 3, NG):
            step(At(n // SLOTS, n % SLOTS))

    with ExitStack() as ctx:
        def sb(name, shape, dt):
            return ctx.enter_context(nc.sbuf_tensor(name, shape, dt))

        def ps(name, shape, dt=F32):
            return ctx.enter_context(nc.psum_tensor(name, shape, dt))

        def sem(name):
            return ctx.enter_context(nc.semaphore(name))

        q_stack = [sb(f"b_q_stack{s}", [P, GH, SEQ], BF16) for s in range(SLOTS)]
        k_stack = [sb(f"b_k_stack{s}", [P, SEQ], BF16) for s in range(SLOTS)]
        v_here = [sb(f"b_v_here{s}", [P, ST, 2 * HD], F32) for s in range(SLOTS)]
        probs = sb("b_probs", [P, PRING, GH, HALF], F32)
        mask = sb("b_mask", [P, SEQ], BF16)
        future = sb("b_future", [P, P], BF16)
        ident = sb("b_ident", [P, P], BF16)
        masked = sb("b_masked", [P, 4, SEQ], BF16)
        maxima = sb("b_maxima", [P, SLOTS, UNITS], F32)
        max_rest = sb("b_max_rest", [P, 2, UNITS], F32)
        neg_max = sb("b_neg_max", [P, PARTS, UNITS], BF16)
        neg_max_t = sb("b_neg_max_t", [PARTS * UNITS, P], BF16)
        o_sb = sb("b_o_sb", [P, 2, HALF], F32)

        max_ps = ps("b_max_ps", [P, 2 * SEQ])
        exp_ps = ps("b_exp_ps", [P, ERING, HALF])
        o_ps = ps("b_o_ps", [P, HALF])
        turn_ps = max_ps[0:PARTS * UNITS, 0:P // 2].bitcast(BF16)

        ones_set = sem("b_ones_set")
        mask_set = sem("b_mask_set")
        ident_set = sem("b_ident_set")
        stack_in = [sem(f"b_stack_in{s}") for s in range(SLOTS)]
        scores_max = sem("b_scores_max")
        max_read = sem("b_max_read")
        neg_done = sem("b_neg_done")
        turned = sem("b_turned")
        turn_copied = sem("b_turn_copied")
        neg_in = sem("b_neg_in")
        scores_exp = sem("b_scores_exp")
        exp_done = sem("b_exp_done")
        pv_done = sem("b_pv_done")
        o_copied = sem("b_o_copied")
        dve_passed = sem("b_dve_passed")
        pool_passed = sem("b_pool_passed")
        o_stored = [sem(f"b_o_stored{s}") for s in range(2)]

        block = ctx.enter_context(nc.Block())
        LOADS = 2 * PARTS * (PARTS + 1) // 2 + 1
        SPLIT = 5

        @block.sync
        def _(sp):
            def load(g):
                done = stack_in[g.slot]
                rows = 0
                for m in range(PARTS):
                    copies = PARTS - m
                    for r in range(copies):
                        sp.dma_start(q_stack[g.slot][rows + r * HD:rows + (r + 1) * HD, :, :],
                                     q_parts[m, bass.ds(g.n * GH * HD, GH * HD), :].rearrange("(h d) t -> d h t", d=HD)
                                     ).then_inc(done, 16)
                        sp.dma_start(k_stack[g.slot][rows + r * HD:rows + (r + 1) * HD, :],
                                     k_parts[r, bass.ds(g.n * HD, HD), :]).then_inc(done, 16)
                    rows += copies * HD
                sp.dma_start(v_here[g.slot][:, :, :], v_all[:, bass.ds(g.n, 1), :, :].rearrange("p a j d -> p (a j) d")
                             ).then_inc(done, 16)

            def neg_rows(g):
                sp.wait_ge(turn_copied, g.n + 1)
                for m in range(PARTS):
                    sp.dma_start(q_stack[g.slot][STACK + m:STACK + m + 1, :, :].rearrange("m h (i t) -> m (h i) t", t=P),
                                 neg_max_t[m * UNITS:(m + 1) * UNITS, :]).then_inc(neg_in, 16)

            def store(g, hf):
                sp.wait_ge(o_copied, 2 * g.n + hf + 1)
                sp.dma_start(o_rows[bass.ds(g.n, 1), :, hf * HALF:(hf + 1) * HALF].rearrange("a p t -> (a p) t"),
                             o_sb[:, hf, :]).then_inc(o_stored[hf], 16)

            def step(g):
                if g.has(2):
                    wait(sp, pv_done, NC * g.n)
                    load(g.next(2))
                if not (isinstance(g.n, int) and g.n == 0):
                    store(g.next(-1), 1)
                store(g, 0)
                if g.has(1):
                    neg_rows(g.next(1))

            load(At(0, 0))
            load(At(0, 1))
            neg_rows(At(0, 0))
            over_groups(sp, step)
            store(At(0, NG - 1), 1)
            sp.wait_ge(o_stored[0], 16 * NG)
            sp.wait_ge(o_stored[1], 16 * NG)

        @block.gpsimd
        def _(pool):
            for s in range(SLOTS):
                pool.memset(k_stack[s][STACK:STACKM, :], 1.0).then_inc(ones_set, 1)
            pool.wait_ge(ones_set, SLOTS)
            pool.memset(mask[:, :], 0.0).then_inc(mask_set, 1)
            pool.wait_ge(mask_set, 1)
            pool.affine_select(out=mask[:, SEQ - P:], in_=mask[:, SEQ - P:], compare_op=ALU.is_ge, fill=NEG, base=0,
                               pattern=[[-1, P]], channel_multiplier=1).then_inc(mask_set, 1)
            pool.memset(future[:, :], 0.0).then_inc(mask_set, 1)
            pool.wait_ge(mask_set, 3)
            pool.affine_select(out=future[:, :], in_=future[:, :], compare_op=ALU.is_ge, fill=NEG, base=0,
                               pattern=[[1, P]], channel_multiplier=-1).then_inc(mask_set, 1)
            identity(pool, ident_set, ident, 0)

            def split(g):
                mx, rs, ng = maxima[:, g.slot, :], max_rest, neg_max
                base = SPLIT * g.n
                pool.wait_ge(max_read, UNITS * (g.n + 1))
                wait_apart(pool, turned, g.n, pool_passed)
                pool.tensor_scalar(ng[:, 0, :], mx, -1.0, None, ALU.mult).then_inc(neg_done, 1)
                wait_apart(pool, neg_done, base + 1, pool_passed)
                pool.tensor_tensor(rs[:, 0, :], mx, ng[:, 0, :], ALU.add).then_inc(neg_done, 1)
                wait_apart(pool, neg_done, base + 2, pool_passed)
                pool.tensor_scalar(ng[:, 1, :], rs[:, 0, :], -1.0, None, ALU.mult).then_inc(neg_done, 1)
                wait_apart(pool, neg_done, base + 3, pool_passed)
                pool.tensor_tensor(rs[:, 1, :], rs[:, 0, :], ng[:, 1, :], ALU.add).then_inc(neg_done, 1)
                wait_apart(pool, neg_done, base + 4, pool_passed)
                pool.tensor_scalar(ng[:, 2, :], rs[:, 1, :], -1.0, None, ALU.mult).then_inc(neg_done, 1)

            split(At(0, 0))

            def step(g):
                if g.has(1):
                    split(g.next(1))

            over_groups(pool, step)

        @block.scalar
        def _(act):
            def copy_turn(g):
                act.wait_ge(turned, g.n + 1)
                wait(act, neg_in, 16 * PARTS * g.n)
                act.activation(neg_max_t[:, :], turn_ps, ACT.Copy).then_inc(turn_copied, 1)

            def copy_o(g, hf):
                act.wait_ge(pv_done, NC * g.n + (NC if hf else ST // 2))
                wait(act, o_stored[hf], 16 * g.n)
                act.activation(o_sb[:, hf, :], o_ps[:, :], ACT.Copy).then_inc(o_copied, 1)

            def step(g):
                for c in range(NC):
                    q0, w = start_of(c)
                    for h in range(GH):
                        i = c * GH + h
                        act.wait_ge(scores_exp, GH * NC * g.n + i + 1)
                        if h == 0:
                            wait(act, pv_done, NC * g.n + c - PRING + 1)
                        act.activation(probs[:, c % PRING, h, 0:w], exp_ps[:, i % ERING, 0:w], ACT.Exp,
                                       scale=SCALE).then_inc(exp_done, 1)
                        if i == TURN_AT and g.has(1):
                            copy_turn(g.next(1))
                    if c == 1 and not (isinstance(g.n, int) and g.n == 0):
                        copy_o(g.next(-1), 1)
                    if c == ST // 2 + 1:
                        copy_o(g, 0)

            copy_turn(At(0, 0))
            over_groups(act, step)
            copy_o(At(0, NG - 1), 1)

        @block.vector
        def _(dve):
            dve.wait_ge(mask_set, 2)

            def unit(g, u):
                i, h = unit_of(u)
                w = P * (i + 1)
                b0 = HALF * banks_of(u)[0]
                dve.wait_ge(scores_max, UNITS * g.n + u + 1)
                wait_apart(dve, max_read, UNITS * g.n + u - 3, dve_passed)
                dve.tensor_tensor_reduce(masked[:, u % 4, 0:w], max_ps[:, b0:b0 + w], mask[:, SEQ - w:], 1.0, NEG,
                                         ALU.add, ALU.max, maxima[:, g.slot, h * ST + i:h * ST + i + 1]).then_inc(max_read, 1)

            for u in range(UNITS):
                unit(At(0, 0), u)
            for u in range(AHEAD):
                unit(At(0, 1), u)

            def step(g):
                for here in PLAN:
                    for kind, by, u in here:
                        if kind == "u" and g.has(by):
                            unit(g.next(by), u)

            over_groups(dve, step)

        @block.tensor
        def _(pe):
            def stacked(g):
                pe.wait_ge(stack_in[g.slot], 16 * LOADS * (g.turn + 1))

            def max_scores(g, u):
                i, h = unit_of(u)
                if u == 0:
                    stacked(g)
                wait(pe, max_read, UNITS * g.n + room_at(u))
                if u == TURN:
                    wait(pe, turn_copied, g.n)
                w = P * (i + 1)
                b0 = HALF * banks_of(u)[0]
                for k0 in range(0, w, HALF):
                    n = min(HALF, w - k0)
                    mm = pe.matmul(max_ps[:, b0 + k0:b0 + k0 + n], q_stack[g.slot][0:STACK, h, i * P:(i + 1) * P],
                                   k_stack[g.slot][0:STACK, k0:k0 + n], start=True, stop=True)
                mm.then_inc(scores_max, 1)

            def turn(g, after):
                pe.wait_ge(neg_done, SPLIT * (g.n + 1))
                if after is not None:
                    pe.wait_ge(max_read, UNITS * after.n + TURN - 1)
                pe.transpose(turn_ps, neg_max[:, :, :].rearrange("p m u -> p (m u)"), ident[:, :]).then_inc(turned, 1)

            def exp_scores(g, c, h):
                hf, j = CHUNKS[c]
                q0, w = start_of(c)
                i = c * GH + h
                if i == 0:
                    pe.wait_ge(neg_in, 16 * PARTS * (g.n + 1))
                wait(pe, exp_done, GH * NC * g.n + i - ERING + 1)
                mm = pe.matmul(exp_ps[:, i % ERING, 0:w], k_stack[g.slot][0:STACKM, j * P:(j + 1) * P],
                               q_stack[g.slot][0:STACKM, h, q0:q0 + w], start=True, stop=c not in DIAG)
                if c in DIAG:
                    mm = pe.matmul(exp_ps[:, i % ERING, 0:P], ident[:, :], future[:, :], start=False, stop=True)
                mm.then_inc(scores_exp, 1)

            def times_values(g, c):
                hf, j = CHUNKS[c]
                q0, w = start_of(c)
                pe.wait_ge(exp_done, GH * (NC * g.n + c + 1))
                if j == 0:
                    wait(pe, o_copied, 2 * g.n + hf)
                o0 = q0 - hf * HALF
                for h in range(GH):
                    mm = pe.matmul(o_ps[h * 2 * HD:(h + 1) * 2 * HD, o0:o0 + w], v_here[g.slot][:, j, :],
                                   probs[:, c % PRING, h, 0:w], start=(j == 0), stop=(j == (hf + 1) * ST // 2 - 1),
                                   skip_group_check=True)
                mm.then_inc(pv_done, 1)

            def step(g):
                for c in range(NC):
                    for h in range(GH):
                        exp_scores(g, c, h)
                        for kind, by, u in PLAN[c * GH + h]:
                            if kind == "u" and g.has(by):
                                max_scores(g.next(by), u)
                            if kind == "t" and g.has(by):
                                turn(g.next(by), g.next(by + 1) if g.has(by + 1) else None)
                    if c >= 2:
                        times_values(g, c - 2)
                    elif not (isinstance(g.n, int) and g.n == 0):
                        times_values(g.next(-1), NC + c - 2)

            pe.wait_ge(ones_set, SLOTS)
            pe.wait_ge(mask_set, 4)
            pe.wait_ge(ident_set, 2)
            for u in range(UNITS):
                max_scores(At(0, 0), u)
            for u in range(TURN):
                max_scores(At(0, 1), u)
            turn(At(0, 0), At(0, 1))
            for u in range(TURN, AHEAD):
                max_scores(At(0, 1), u)
            over_groups(pe, step)
            times_values(At(0, NG - 1), NC - 2)
            times_values(At(0, NG - 1), NC - 1)


def split_weights(pool, pieces, loaded, hi_ready, lo_ready):
    def load(k):
        wait(pool, lo_ready, k - 1)
        pool.dma_start(pieces[k][1], pieces[k][0]).then_inc(loaded[k % 2], 16)

    load(0)
    for k, (_, raw, hi, lo) in enumerate(pieces):
        if k + 1 < len(pieces):
            load(k + 1)
        pool.wait_ge(loaded[k % 2], 16 * (k // 2 + 1))
        pool.tensor_copy(hi, raw).then_inc(hi_ready, 1)
        pool.wait_ge(hi_ready, k + 1)
        pool.tensor_tensor(lo, raw, hi.bitcast(F32), ALU.subtract).then_inc(lo_ready, 1)


def phase_c(nc, x, wo_t, o_rows, x1, xn_t, wgu_t, w_up):
    XRING = 4
    with ExitStack() as ctx:
        def sb(name, shape, dt):
            return ctx.enter_context(nc.sbuf_tensor(name, shape, dt))

        def ps(name, shape):
            return ctx.enter_context(nc.psum_tensor(name, shape, F32))

        def sem(name):
            return ctx.enter_context(nc.semaphore(name))

        w_raw = sb("c_w_raw", [P, KT, HID], F32)
        w_hi = sb("c_w_hi", [P, KT, HID], F32R)
        w_lo = sb("c_w_lo", [P, KT, HID], F32R)
        ident = sb("c_ident", [P, P], F32)
        up_raw = sb("c_up_raw", [P, 2, INTER], F32)
        eps = sb("c_eps", [P, 1], F32)
        o_in = sb("c_o_in", [P, 2, NKV, P], F32)
        x_in = sb("c_x_in", [P, XRING, HID], F32)
        rsum = sb("c_rsum", [P, 2, NH], F32)
        attn = sb("c_attn", [P, 2, HID], F32)
        attn_hi = sb("c_attn_hi", [P, 2, HID], F32R)
        attn_lo = sb("c_attn_lo", [P, 2, HID], F32R)
        x1_sb = sb("c_x1_sb", [P, 2, HID], F32)
        stats = sb("c_stats", [P, 2, 6], F32)
        mean_var = sb("c_mean_var", [P, 2, 2], F32)
        std = sb("c_std", [P, 2, 1], F32)
        rstd = sb("c_rstd", [P, 2, 1], F32)
        xn = sb("c_xn", [P, 2, HID], F32)
        xt_sb = sb("c_xt_sb", [P, 2, HID], F32)

        ot_ps = ps("c_ot_ps", [P, 2, 1024])
        at_ps = ps("c_at_ps", [P, HID])
        y_ps = ps("c_y_ps", [P, HID])
        xt_ps = ps("c_xt_ps", [P, HID])

        w_in = sem("c_w_in")
        o_loaded = [sem(f"c_o_loaded{s}") for s in range(2)]
        x_loaded = [sem(f"c_x_loaded{s}") for s in range(2)]
        x1_stored = [sem(f"c_x1_stored{s}") for s in range(2)]
        xt_stored = [sem(f"c_xt_stored{s}") for s in range(2)]
        pool_const = sem("c_pool_const")
        w_hi_ready = sem("c_w_hi_ready")
        w_lo_ready = sem("c_w_lo_ready")
        ot_done = sem("c_ot_done")
        rsum_done = sem("c_rsum_done")
        attn_done = sem("c_attn_done")
        at_done = sem("c_at_done")
        attn_hi_done = sem("c_attn_hi_done")
        attn_lo_done = sem("c_attn_lo_done")
        y_done = sem("c_y_done")
        x1_done = sem("c_x1_done")
        stats_done = sem("c_stats_done")
        var_done = sem("c_var_done")
        std_done = sem("c_std_done")
        rstd_done = sem("c_rstd_done")
        xn_done = sem("c_xn_done")
        xt_done = sem("c_xt_done")
        xt_copied = sem("c_xt_copied")
        passed = sem("c_passed")
        up_loaded = [sem(f"c_up_loaded{s}") for s in range(2)]
        up_hi_ready = sem("c_up_hi_ready")
        up_lo_ready = sem("c_up_lo_ready")

        block = ctx.enter_context(nc.Block())

        def tok(t):
            return bass.ds(t * P, P)

        def twice(s, t):
            return 16 * (t // 2 + 1) if isinstance(t, int) else 8 * (t - s) + 16

        @block.sync
        def _(sp):
            def load_o(t, s):
                wait(sp, ot_done, t - 1)
                if isinstance(t, int):
                    b, i = t // ST, t % ST
                    sp.dma_start(o_in[:, s, :, :], o_rows[b * NKV:(b + 1) * NKV, :, i * P:(i + 1) * P].rearrange("g p t -> p g t")
                                 ).then_inc(o_loaded[s], 16)
                else:
                    sp.dma_start(o_in[:, s, :, :], o_rows[bass.ds(t // ST * NKV, NKV), :, bass.ds(t % ST * P, P)].rearrange("g p t -> p g t")
                                 ).then_inc(o_loaded[s], 16)

            def load_x(t, s):
                wait(sp, x1_done, t - XRING + 1)
                sp.dma_start(x_in[:, bass.ds(t % XRING, 1), :].rearrange("p a n -> p (a n)"), x[tok(t), :]).then_inc(x_loaded[s], 16)

            def step(t, s):
                if exists(t + 2):
                    load_o(t + 2, s)
                    load_x(t + 2, s)
                if isinstance(t, int) and t == -1:
                    sp.dma_start(w_raw[:, :, :], wo_t.rearrange("(k p) n -> p k n", p=P)).then_inc(w_in, 16)

            over_tiles(sp, step)
            for s in range(2):
                sp.wait_ge(x1_stored[s], 8 * TT)
                sp.wait_ge(xt_stored[s], 8 * TT)

        @block.gpsimd
        def _(pool):
            identity(pool, pool_const, ident, 0)
            pool.memset(eps[:, :], EPS).then_inc(pool_const, 1)
            up_hi, up_lo = w_up
            split_weights(pool, [(wgu_t[k * P:(k + 1) * P, :], up_raw[:, k % 2, :], up_hi[:, k, :], up_lo[:, k, :])
                                 for k in range(2 * KT)], up_loaded, up_hi_ready, up_lo_ready)

        @block.scalar
        def _(act):
            act.wait_ge(pool_const, 3)

            def hi(t, s):
                act.wait_ge(at_done, t + 1)
                wait(act, y_done, t - 1)
                act.activation(attn_hi[:, s, :], at_ps[:, :], ACT.Copy).then_inc(attn_hi_done, 1)

            def std_of(t, s):
                act.wait_ge(var_done, t + 1)
                wait(act, rstd_done, t - 1)
                act.activation(std[:, s, :], mean_var[:, s, 1:2], ACT.Sqrt, bias=eps[:, :]).then_inc(std_done, 1)

            def out(t, s):
                act.wait_ge(xt_done, t + 1)
                if isinstance(t, int):
                    wait(act, xt_stored[s], 16 * (t // 2))
                else:
                    act.wait_ge(xt_stored[s], 8 * (t - s))
                act.activation(xt_sb[:, s, :], xt_ps[:, :], ACT.Copy).then_inc(xt_copied, 1)

            def store_x1(t, s):
                act.wait_ge(x1_done, t + 1)
                act.dma_start(x1[tok(t), :], x1_sb[:, s, :]).then_inc(x1_stored[s], 16)

            def store_xt(t, s):
                act.wait_ge(xt_copied, t + 1)
                act.dma_start(xn_t[:, tok(t)].rearrange("(k p) t -> p k t", p=P),
                              xt_sb[:, s, :].rearrange("p (k t) -> p k t", k=KT)).then_inc(xt_stored[s], 16)

            def step(t, s):
                if exists(t + 1):
                    hi(t + 1, 1 - s)
                if isinstance(t, int) and t == -1:
                    act.wait_ge(w_in, 16)
                    for k in range(KT):
                        act.activation(w_hi[:, k, :], w_raw[:, k, :], ACT.Copy).then_inc(w_hi_ready, 1)
                if exists(t - 1):
                    out(t - 1, 1 - s)
                if exists(t):
                    std_of(t, s)
                    store_x1(t, s)
                if exists(t - 1):
                    store_xt(t - 1, 1 - s)

            over_tiles(act, step)

        @block.vector
        def _(dve):
            def divide(t, s):
                dve.wait_ge(ot_done, t + 1)
                wait(dve, at_done, t - 1)
                wait(dve, attn_done, t - 1)
                rows = ot_ps[:, s, :].rearrange("p (h r) -> p h r", r=2 * HD)
                dve.reciprocal(rsum[:, s, :].unsqueeze(2), rows[:, :, HD:HD + 1]).then_inc(rsum_done, 1)
                dve.wait_ge(rsum_done, t + 1)
                dve.tensor_tensor(attn[:, s, :].rearrange("p (h d) -> p h d", d=HD), rows[:, :, 0:HD],
                                  rsum[:, s, :].unsqueeze(2).to_broadcast([P, NH, HD]), ALU.mult).then_inc(attn_done, 1)

            def lo(t, s):
                dve.wait_ge(attn_hi_done, t + 1)
                dve.tensor_tensor(attn_lo[:, s, :], at_ps[:, :], attn_hi[:, s, :].bitcast(F32),
                                  ALU.subtract).then_inc(attn_lo_done, 1)

            def residual(t, s):
                dve.wait_ge(y_done, t + 1)
                dve.wait_ge(x_loaded[s], twice(s, t))
                if isinstance(t, int):
                    wait(dve, x1_stored[s], 16 * (t // 2))
                else:
                    dve.wait_ge(x1_stored[s], 8 * (t - s))
                wait(dve, xn_done, t - 1)
                dve.tensor_tensor(x1_sb[:, s, :], y_ps[:, :], x_in[:, bass.ds(t % XRING, 1), :].rearrange("p a n -> p (a n)"), ALU.add).then_inc(x1_done, 1)
                dve.wait_ge(x1_done, t + 1)
                wait(dve, std_done, t - 1)
                dve.bn_stats(stats[:, s, :], x1_sb[:, s, :]).then_inc(stats_done, 1)
                wait_apart(dve, stats_done, t + 1, passed)
                dve.bn_aggr(mean_var[:, s, :], stats[:, s, :]).then_inc(var_done, 1)

            def normalise(t, s):
                dve.wait_ge(std_done, t + 1)
                dve.reciprocal(rstd[:, s, :], std[:, s, :]).then_inc(rstd_done, 1)
                dve.wait_ge(rstd_done, t + 1)
                wait(dve, xt_done, t - 1)
                dve.tensor_scalar(xn[:, s, :], x1_sb[:, s, :], mean_var[:, s, 0:1], rstd[:, s, :],
                                  ALU.subtract, ALU.mult).then_inc(xn_done, 1)

            def step(t, s):
                if exists(t + 2):
                    divide(t + 2, s)
                if exists(t + 1):
                    lo(t + 1, 1 - s)
                if isinstance(t, int) and t == -1:
                    for k in range(KT):
                        dve.wait_ge(w_hi_ready, k + 1)
                        dve.tensor_tensor(w_lo[:, k, :], w_raw[:, k, :], w_hi[:, k, :].bitcast(F32),
                                          ALU.subtract).then_inc(w_lo_ready, 1)
                if exists(t):
                    residual(t, s)
                    normalise(t, s)

            over_tiles(dve, step)

        @block.tensor
        def _(pe):
            def o_transposes(t, s):
                pe.wait_ge(o_loaded[s], twice(s, t))
                wait(pe, attn_done, t - 1)
                for g in range(NKV):
                    mm = pe.transpose(ot_ps[:, s, g * P:(g + 1) * P], o_in[:, s, g, :], ident[:, :])
                mm.then_inc(ot_done, 1)

            def a_transposes(t, s):
                pe.wait_ge(attn_done, t + 1)
                wait(pe, attn_lo_done, t)
                for k in range(KT):
                    mm = pe.transpose(at_ps[:, k * P:(k + 1) * P], attn[:, s, k * P:(k + 1) * P], ident[:, :])
                mm.then_inc(at_done, 1)

            def products(t, s):
                pe.wait_ge(attn_lo_done, t + 1)
                wait(pe, x1_done, t)
                n = 0
                for k in range(KT):
                    for a, w in ((attn_hi, w_hi), (attn_hi, w_lo), (attn_lo, w_hi)):
                        mm = pe.matmul(y_ps[:, :], a[:, s, k * P:(k + 1) * P], w[:, k, :],
                                       start=(n == 0), stop=(n == 3 * KT - 1))
                        n += 1
                mm.then_inc(y_done, 1)

            def x_transposes(t, s):
                pe.wait_ge(xn_done, t + 1)
                wait(pe, xt_copied, t)
                for k in range(KT):
                    mm = pe.transpose(xt_ps[:, k * P:(k + 1) * P], xn[:, s, k * P:(k + 1) * P], ident[:, :])
                mm.then_inc(xt_done, 1)

            def step(t, s):
                if exists(t + 2):
                    o_transposes(t + 2, s)
                if exists(t + 1):
                    a_transposes(t + 1, 1 - s)
                if exists(t):
                    if isinstance(t, int) and t == 0:
                        pe.wait_ge(w_lo_ready, KT)
                    products(t, s)
                if exists(t - 1):
                    x_transposes(t - 1, 1 - s)

            pe.wait_ge(pool_const, 2)
            over_tiles(pe, step)


def phase_d(nc, w_up, wd_t, x1, xn_t, out):
    CT = 4
    CW = CT * P
    NCH = TT // CT
    SPLIT_AT = 4

    def rows(i):
        return min(P, INTER - i * P)

    with ExitStack() as ctx:
        def sb(name, shape, dt):
            return ctx.enter_context(nc.sbuf_tensor(name, shape, dt))

        def ps(name, shape):
            return ctx.enter_context(nc.psum_tensor(name, shape, F32))

        def sem(name):
            return ctx.enter_context(nc.semaphore(name))

        up_hi, up_lo = w_up
        wd_raw = sb("d_wd_raw", [P, 2, HID], F32)
        wd_hi = sb("d_wd_hi", [P, IT, HID], F32R)
        wd_lo = sb("d_wd_lo", [P, IT, HID], F32R)
        xn_hi = sb("d_xn_hi", [P, 2, KT, CW], F32R)
        xn_raw = sb("d_xn_raw", [P, KT, CW], F32)
        xn_lo = sb("d_xn_lo", [P, 2, KT, CW], F32R)
        y_sb = sb("d_y_sb", [P, CT, HID], F32)
        gate = sb("d_gate", [P, 2, CW], F32)
        prod = sb("d_prod", [P, CW], F32)
        h_hi = sb("d_h_hi", [P, 2, CW], F32R)
        h_lo = sb("d_h_lo", [P, 2, CW], F32R)

        g_ps = ps("d_g_ps", [P, 2, CW])
        u_ps = ps("d_u_ps", [P, 2, CW])
        y_ps = ps("d_y_ps", [P, CT, HID])

        wd_loaded = [sem(f"d_wd_loaded{s}") for s in range(2)]
        wd_hi_ready = sem("d_wd_hi_ready")
        wd_lo_ready = sem("d_wd_lo_ready")
        xn_in = sem("d_xn_in")
        x1_loaded = sem("d_x1_loaded")
        xn_hi_done = sem("d_xn_hi_done")
        xn_lo_done = sem("d_xn_lo_done")
        g_done = sem("d_g_done")
        u_done = sem("d_u_done")
        gate_done = sem("d_gate_done")
        prod_done = sem("d_prod_done")
        h_hi_done = sem("d_h_hi_done")
        h_lo_done = sem("d_h_lo_done")
        y_step = sem("d_y_step")
        out_done = sem("d_out_done")
        out_stored = sem("d_out_stored")

        block = ctx.enter_context(nc.Block())

        def over_chunks(engine, chunk):
            chunk(0)
            with engine.Fori(1, NCH - 1) as c:
                chunk(c)
            chunk(NCH - 1)

        def is_first(c):
            return isinstance(c, int) and c == 0

        def has_next(c):
            return not isinstance(c, int) or c + 1 < NCH

        def slot(tensor, c, k):
            if isinstance(c, int):
                return tensor[:, c % 2, k, :]
            return tensor[:, bass.ds(c % 2, 1), k, :].rearrange("p a t -> p (a t)")

        def two_back(n, i):
            return n if i == 0 and IT % 2 else n - 1

        @block.sync
        def _(sp):
            def load_xn(c):
                wait(sp, xn_lo_done, KT * c)
                sp.dma_start(xn_raw[:, :, :], xn_t[:, bass.ds(c * CW, CW)].rearrange("(k p) t -> p k t", p=P)).then_inc(xn_in, 16)

            def load_x1(c):
                wait(sp, out_stored, 16 * CT * c)
                sp.dma_start(y_sb[:, :, :], x1[bass.ds(c * CW, CW), :].rearrange("(a p) n -> p a n", p=P)).then_inc(x1_loaded, 16)

            def store(c):
                for a in range(CT):
                    sp.wait_ge(out_done, CT * c + a + 1)
                    sp.dma_start(out[bass.ds(c * CW + a * P, P), :], y_sb[:, a, :]).then_inc(out_stored, 16)

            def chunk(c):
                if has_next(c):
                    load_xn(c + 1)
                if not is_first(c):
                    store(c - 1)
                load_x1(c)

            load_xn(0)
            over_chunks(sp, chunk)
            store(NCH - 1)
            sp.wait_ge(out_stored, 16 * CT * NCH)

        @block.gpsimd
        def _(pool):
            split_weights(pool, [(wd_t[i * P:i * P + rows(i), :], wd_raw[0:rows(i), i % 2, :],
                                  wd_hi[0:rows(i), i, :], wd_lo[0:rows(i), i, :]) for i in range(IT)],
                          wd_loaded, wd_hi_ready, wd_lo_ready)

        @block.scalar
        def _(act):
            def split_xn(c, k):
                act.wait_ge(xn_in, 16 * (c + 1))
                wait(act, u_done, IT * (c - 1))
                act.activation(slot(xn_hi, c, k), xn_raw[:, k, :], ACT.Copy).then_inc(xn_hi_done, 1)

            def silu(c, i):
                n = IT * c + i
                r = rows(i)
                act.wait_ge(g_done, n + 1)
                wait(act, prod_done, two_back(n, i))
                act.activation(gate[0:r, i % 2, :], g_ps[0:r, i % 2, :], ACT.Silu).then_inc(gate_done, 1)

            def hi(c, i):
                n = IT * c + i
                r = rows(i)
                act.wait_ge(prod_done, n + 1)
                wait(act, y_step, two_back(n, i))
                act.activation(h_hi[0:r, i % 2, :], prod[0:r, :], ACT.Copy).then_inc(h_hi_done, 1)

            def chunk(c):
                for i in range(IT):
                    silu(c, i)
                    if i >= 1:
                        hi(c, i - 1)
                    elif not is_first(c):
                        hi(c - 1, IT - 1)
                    if has_next(c) and 0 <= i - SPLIT_AT < KT:
                        split_xn(c + 1, i - SPLIT_AT)

            for k in range(KT):
                split_xn(0, k)
            over_chunks(act, chunk)
            hi(NCH - 1, IT - 1)

        @block.vector
        def _(dve):
            def split_xn(c, k):
                dve.wait_ge(xn_hi_done, KT * c + k + 1)
                wait(dve, u_done, IT * (c - 1))
                dve.tensor_tensor(slot(xn_lo, c, k), xn_raw[:, k, :], slot(xn_hi, c, k).bitcast(F32),
                                  ALU.subtract).then_inc(xn_lo_done, 1)

            def product(c, i):
                n = IT * c + i
                r = rows(i)
                dve.wait_ge(gate_done, n + 1)
                dve.wait_ge(u_done, n + 1)
                wait(dve, h_lo_done, n)
                dve.tensor_tensor(prod[0:r, :], u_ps[0:r, i % 2, :], gate[0:r, i % 2, :], ALU.mult).then_inc(prod_done, 1)

            def lo(c, i):
                n = IT * c + i
                r = rows(i)
                dve.wait_ge(h_hi_done, n + 1)
                wait(dve, y_step, two_back(n, i))
                dve.tensor_tensor(h_lo[0:r, i % 2, :], prod[0:r, :], h_hi[0:r, i % 2, :].bitcast(F32),
                                  ALU.subtract).then_inc(h_lo_done, 1)

            def add(c):
                dve.wait_ge(x1_loaded, 16 * (c + 1))
                dve.wait_ge(y_step, IT * (c + 1))
                for a in range(CT):
                    dve.tensor_tensor(y_sb[:, a, :], y_ps[:, a, :], y_sb[:, a, :], ALU.add).then_inc(out_done, 1)

            def chunk(c):
                for i in range(IT):
                    product(c, i)
                    if i == 0 and not is_first(c):
                        add(c - 1)
                    lo(c, i)
                    if has_next(c) and 0 <= i - SPLIT_AT < KT:
                        split_xn(c + 1, i - SPLIT_AT)

            for k in range(KT):
                split_xn(0, k)
            over_chunks(dve, chunk)
            add(NCH - 1)

        @block.tensor
        def _(pe):
            def up(c, i, w, bank, done):
                r = rows(i)
                n = 0
                for k in range(KT):
                    cols = slice(i * P, i * P + r)
                    if i == 0:
                        pe.wait_ge(xn_lo_done, KT * c + k + 1)
                    for a, b in ((up_hi, xn_hi), (up_hi, xn_lo), (up_lo, xn_hi)):
                        mm = pe.matmul(bank[0:r, i % 2, :], a[:, KT * w + k, cols], slot(b, c, k), start=(n == 0), stop=(n == 3 * KT - 1))
                        n += 1
                mm.then_inc(done, 1)

            def down(c, i):
                r = rows(i)
                pe.wait_ge(h_lo_done, IT * c + i + 1)
                if is_first(c) or i == IT - 1:
                    pe.wait_ge(wd_lo_ready, i + 1)
                if i == 0:
                    wait(pe, out_done, CT * c)
                for a in range(CT):
                    toks = slice(a * P, (a + 1) * P)
                    for n, (h, w) in enumerate(((h_hi, wd_hi), (h_hi, wd_lo), (h_lo, wd_hi))):
                        mm = pe.matmul(y_ps[:, a, :], h[0:r, i % 2, toks], w[0:r, i, :],
                                       start=(i == 0 and n == 0), stop=(i == IT - 1 and n == 2))
                mm.then_inc(y_step, 1)

            def chunk(c):
                for i in range(IT):
                    wait(pe, prod_done, two_back(IT * c + i, i))
                    up(c, i, 0, g_ps, g_done)
                    up(c, i, 1, u_ps, u_done)
                    if i >= 1:
                        down(c, i - 1)
                    elif not is_first(c):
                        down(c - 1, IT - 1)

            over_chunks(pe, chunk)
            down(NCH - 1, IT - 1)


def transformer_layer(nc, x, wqkv_t, wo_t, wgu_t, wd_t, cos_t, sin_t, out):
    q_parts = nc.dram_tensor("q_parts", [PARTS, BATCH * QROWS, SEQ], BF16, kind="Internal").ap()
    k_parts = nc.dram_tensor("k_parts", [PARTS, BATCH * KROWS, SEQ], BF16, kind="Internal").ap()
    o_rows = nc.dram_tensor("o_rows", [NG, P, SEQ], F32, kind="Internal").ap()
    x1 = nc.dram_tensor("x1", [TOK, HID], F32, kind="Internal").ap()
    xn_t = nc.dram_tensor("xn_t", [HID, TOK], F32, kind="Internal").ap()
    with nc.sbuf_tensor("v_all", [P, NG, ST, 2 * HD], F32) as v_all:
        phase_a(nc, x, wqkv_t, cos_t, sin_t, q_parts, k_parts, v_all)
        phase_b(nc, q_parts, k_parts, v_all, o_rows)
    with nc.sbuf_tensor("up_hi", [P, 2 * KT, INTER], F32R) as up_hi, nc.sbuf_tensor("up_lo", [P, 2 * KT, INTER], F32R) as up_lo:
        phase_c(nc, x, wo_t, o_rows, x1, xn_t, wgu_t, (up_hi, up_lo))
        phase_d(nc, (up_hi, up_lo), wd_t, x1, xn_t, out)


def kernel(L0_attn_hidden_states, L0_attn_Wq, L0_attn_Wk, L0_attn_Wv, L0_attn_Wo, L0_ffn_w_gate, L0_ffn_w_up,
           L0_ffn_w_down):
    import numpy as np
    import concourse.bacc as bacc
    from concourse.bass_utils import run_bass_kernel_spmd

    inv_freq = (1.0 / np.float32(10000.0) ** (np.arange(0, HD, 2, dtype=np.float32) / np.float32(HD))).astype(np.float32)
    angle = np.outer(np.arange(SEQ, dtype=np.float32), inv_freq).astype(np.float32)
    cos_t = np.concatenate([np.cos(angle), np.cos(angle)], axis=1).astype(np.float32)
    sin_t = np.concatenate([-np.sin(angle), np.sin(angle)], axis=1).astype(np.float32)

    def turned(w):
        return np.ascontiguousarray(np.asarray(w).T)

    arrays = {
        "x": np.ascontiguousarray(np.asarray(L0_attn_hidden_states).reshape(TOK, HID)),
        "wqkv_t": turned(np.concatenate([np.asarray(L0_attn_Wq), np.asarray(L0_attn_Wk), np.asarray(L0_attn_Wv)], axis=0)),
        "wo_t": turned(L0_attn_Wo),
        "wgu_t": np.concatenate([turned(L0_ffn_w_gate), turned(L0_ffn_w_up)], axis=0),
        "wd_t": turned(L0_ffn_w_down),
        "cos_t": cos_t,
        "sin_t": sin_t,
    }
    nc = bacc.Bacc("TRN2", target_bir_lowering=False, num_devices=1)
    args = [nc.dram_tensor(f"in_{name}", a.shape, mybir.dt.from_np(a.dtype), kind="ExternalInput").ap()
            for name, a in arrays.items()]
    out = nc.dram_tensor("out_0", (TOK, HID), F32, kind="ExternalOutput").ap()
    transformer_layer(nc, *args, out)
    r = run_bass_kernel_spmd(nc, [{f"in_{name}": a for name, a in arrays.items()}], core_ids=[0])
    return r.results[0]["out_0"].reshape(BATCH, SEQ, HID)
```

```python
from contextlib import ExitStack

import concourse.bass as bass
from concourse import mybir

ALU = mybir.AluOpType
ACT = mybir.ActivationFunctionType
F32 = mybir.dt.float32
F32R = mybir.dt.float32r
BF16 = mybir.dt.bfloat16

P = 128
HID = 512
KT = HID // P
BATCH, SEQ = 2, 1024
TOK = BATCH * SEQ
TT = TOK // P
ST = SEQ // P
NH, NKV = 32, 8
HD = HID // NH
GH = NH // NKV
QROWS, KROWS = NH * HD, NKV * HD
QK = QROWS + KROWS
QKV = QK + KROWS
QKT = QK // P
NG = BATCH * NKV
PARTS = 3
STACK = 6 * HD
STACKM = STACK + PARTS
INTER = 1376
IT = -(-INTER // P)
CT = 4
CW = CT * P
EPS = 1e-5
SCALE = HD ** -0.5
NEG = -3.0e38


def wait(engine, sem, value):
    if not (isinstance(value, int) and value <= 0):
        engine.wait_ge(sem, value)


def wait_apart(engine, sem, value, passed):
    if not (isinstance(value, int) and value <= 0):
        engine.wait_ge(sem, value)
        if not isinstance(value, int):
            engine.sem_inc(passed, 1)


def identity(engine, sem, tensor, n):
    engine.memset(tensor[:, :], 0.0).then_inc(sem, 1)
    engine.wait_ge(sem, n + 1)
    engine.affine_select(out=tensor[:, :], in_=tensor[:, :], compare_op=ALU.not_equal, fill=1.0, base=0,
                         pattern=[[-1, P]], channel_multiplier=1).then_inc(sem, 1)


def over_tiles(engine, step):
    for t in range(-2, 4):
        step(t, t % 2)
    with engine.Fori(2, TT // 2 - 1) as pair:
        step(2 * pair, 0)
        step(2 * pair + 1, 1)
    for t in range(TT - 2, TT + 2):
        step(t, t % 2)


def exists(t):
    return not isinstance(t, int) or 0 <= t < TT


class Between:
    def __init__(self, nc, ctx):
        self.nc, self.ctx = nc, ctx

    def sb(self, name, shape, dt):
        return self.ctx.enter_context(self.nc.sbuf_tensor(name, shape, dt))

    def sem(self, name):
        return self.ctx.enter_context(self.nc.semaphore(name))


class ForB(Between):
    SLOTS = 3
    LOADS = PARTS * (PARTS + 1) + 1

    def __init__(self, nc, ctx):
        super().__init__(nc, ctx)
        self.v_all = self.sb("v_all", [P, NG, ST, 2 * HD], F32)
        self.parts = self.sb("parts", [P, PARTS, QKT, TOK], BF16)
        self.q_stack = [self.sb(f"q_stack{s}", [P, GH, SEQ], BF16) for s in range(self.SLOTS)]
        self.k_stack = [self.sb(f"k_stack{s}", [P, SEQ], BF16) for s in range(self.SLOTS)]
        self.mask = self.sb("mask", [P, SEQ], BF16)
        self.future = self.sb("future", [P, P], BF16)
        self.ident = self.sb("ident", [P, P], BF16)
        self.v_here = [self.sb(f"v_here{s}", [P, ST, 2 * HD], F32) for s in range(self.SLOTS)]
        self.parts_out = [self.sem(f"parts_out{b}") for b in range(BATCH)]
        self.stack_in = [self.sem(f"stack_in{s}") for s in range(self.SLOTS)]

    def constants(self, pool, ones_set, mask_set, ident_set):
        for s in range(self.SLOTS):
            pool.memset(self.k_stack[s][STACK:STACKM, :], 1.0).then_inc(ones_set, 1)
            pool.wait_ge(ones_set, s + 1)
        pool.memset(self.mask[:, :], 0.0).then_inc(mask_set, 1)
        pool.wait_ge(mask_set, 1)
        pool.affine_select(out=self.mask[:, SEQ - P:], in_=self.mask[:, SEQ - P:], compare_op=ALU.is_ge, fill=NEG,
                           base=0, pattern=[[-1, P]], channel_multiplier=1).then_inc(mask_set, 1)
        pool.memset(self.future[:, :], 0.0).then_inc(mask_set, 1)
        pool.wait_ge(mask_set, 3)
        pool.affine_select(out=self.future[:, :], in_=self.future[:, :], compare_op=ALU.is_ge, fill=NEG, base=0,
                           pattern=[[1, P]], channel_multiplier=-1).then_inc(mask_set, 1)
        identity(pool, ident_set, self.ident, 0)

    def load(self, sp, n, slot, q_parts, k_parts):
        done = self.stack_in[slot]
        rows = 0
        for m in range(PARTS):
            for r in range(PARTS - m):
                sp.dma_start(self.q_stack[slot][rows:rows + HD, :, :],
                             q_parts[m, bass.ds(n * GH * HD, GH * HD), :].rearrange("(h d) t -> d h t", d=HD)
                             ).then_inc(done, 16)
                sp.dma_start(self.k_stack[slot][rows:rows + HD, :], k_parts[r, bass.ds(n * HD, HD), :]).then_inc(done, 16)
                rows += HD
        sp.dma_start(self.v_here[slot][:, :, :], self.v_all[:, bass.ds(n, 1), :, :].rearrange("p a j d -> p (a j) d")
                     ).then_inc(done, 16)


class ForC(Between):
    RING = 4

    def __init__(self, nc, ctx):
        super().__init__(nc, ctx)
        self.w_hi = self.sb("wo_hi", [P, KT, HID], F32R)
        self.w_lo = self.sb("wo_lo", [P, KT, HID], F32R)
        self.o_in = self.sb("o_in", [P, self.RING, KT, P], F32)
        self.o_last = self.sb("o_last", [P, SEQ], F32)
        self.o_loaded = [self.sem(f"o_loaded{s}") for s in range(2)]

    def load(self, sp, o_vals, t, s):
        rows = o_vals.rearrange("g r t -> (g r) t")[bass.ds(t // ST * HID, HID), bass.ds(t % ST * P, P)]
        sp.dma_start(self.o_in[:, bass.ds(t % self.RING, 1), :, :].rearrange("p a k t -> p (a k) t"),
                     rows.rearrange("(k p) t -> p k t", p=P)).then_inc(self.o_loaded[s], 16)


class Sums:
    COLS = GH * SEQ // P

    def __init__(self, nc, ctx, phase, o_vals, o_sums, recips):
        self.o_vals, self.o_sums, self.recips = o_vals, o_sums, recips
        self.spread = ctx.enter_context(nc.sbuf_tensor(f"{phase}_sums", [P, self.COLS], F32))
        self.inverted = ctx.enter_context(nc.sbuf_tensor(f"{phase}_inverted", [P, self.COLS], F32))
        self.factors = ctx.enter_context(nc.sbuf_tensor(f"{phase}_factors", [P, SEQ], F32))
        self.sums_out = ctx.enter_context(nc.semaphore(f"{phase}_sums_out"))
        self.sums_in = ctx.enter_context(nc.semaphore(f"{phase}_sums_in"))
        self.inverted_done = ctx.enter_context(nc.semaphore(f"{phase}_inverted_done"))
        self.inverted_out = ctx.enter_context(nc.semaphore(f"{phase}_inverted_out"))
        self.factors_in = ctx.enter_context(nc.semaphore(f"{phase}_factors_in"))
        self.scaled = ctx.enter_context(nc.semaphore(f"{phase}_scaled"))
        self.stored = ctx.enter_context(nc.semaphore(f"{phase}_o_stored"))

    def group(self, dram, n):
        return dram[bass.ds(n, 1), :, :]

    def send(self, sp, o, n, done):
        sp.dma_start(self.group(self.o_sums, n).rearrange("a h t -> (a h) t"), o[HD:P:2 * HD, :]).then_inc(self.sums_out, 16)
        sp.wait_ge(self.sums_out, 16 * (done + 1))
        sp.dma_start(self.spread[:, :], self.group(self.o_sums, n).rearrange("a h (c j) -> (a h c) j", j=self.COLS)
                     ).then_inc(self.sums_in, 16)

    def invert(self, dve, done):
        dve.wait_ge(self.sums_in, 16 * (done + 1))
        wait(dve, self.inverted_out, 16 * done)
        dve.reciprocal(self.inverted[:, :], self.spread[:, :]).then_inc(self.inverted_done, 1)

    def send_inverted(self, sp, n, done):
        sp.wait_ge(self.inverted_done, done + 1)
        sp.dma_start(self.group(self.recips, n).rearrange("a h (c j) -> (a h c) j", j=self.COLS), self.inverted[:, :]
                     ).then_inc(self.inverted_out, 16)

    def fetch_factors(self, sp, n, done):
        wait(sp, self.scaled, done)
        sp.wait_ge(self.inverted_out, 16 * (done + 1))
        for h in range(GH):
            row = self.recips[bass.ds(n, 1), h:h + 1, :].rearrange("a h t -> (a h) t")
            sp.dma_start(self.factors[h * 2 * HD:(h + 1) * 2 * HD, :], row.to_broadcast([2 * HD, SEQ])).then_inc(self.factors_in, 16)

    def scale(self, pool, o, done):
        pool.wait_ge(self.factors_in, 16 * GH * (done + 1))
        pool.tensor_tensor(o, o, self.factors[:, :], ALU.mult).then_inc(self.scaled, 1)

    def store(self, sp, o, n):
        for h in range(GH):
            sp.dma_start(self.o_vals[bass.ds(n, 1), h * HD:(h + 1) * HD, :].rearrange("a p t -> (a p) t"),
                         o[h * 2 * HD:(h * 2 + 1) * HD, :]).then_inc(self.stored, 16)


class ForD(Between):
    def __init__(self, nc, ctx):
        super().__init__(nc, ctx)
        self.up_hi = self.sb("up_hi", [P, 2 * KT, INTER], F32R)
        self.up_lo = self.sb("up_lo", [P, 2 * KT, INTER], F32R)
        self.xn_raw = self.sb("ffn_xn_raw", [P, KT, CW], F32)
        self.xn_hi = self.sb("ffn_xn_hi", [P, 2, KT, CW], F32R)
        self.xn_lo = self.sb("ffn_xn_lo", [P, 2, KT, CW], F32R)


def phase_a(nc, x, wqkv_t, cos_t, sin_t, q_parts, k_parts, for_b, for_c):
    v_all, parts, parts_out = for_b.v_all, for_b.parts, for_b.parts_out
    with ExitStack() as ctx:
        def sb(name, shape, dt):
            return ctx.enter_context(nc.sbuf_tensor(name, shape, dt))

        def ps(name, shape):
            return ctx.enter_context(nc.psum_tensor(name, shape, F32))

        def sem(name):
            return ctx.enter_context(nc.semaphore(name))

        w_raw = for_c.o_in[:, :, :, :].rearrange("p (s a) k t -> p s (a k t)", s=2)[:, :, 0:QKV]
        w_hi = sb("a_w_hi", [P, KT, QKV], F32R)
        w_lo = sb("a_w_lo", [P, KT, QKV], F32R)
        cos = sb("a_cos", [P, TT, HD], F32)
        sin = sb("a_sin", [P, TT, HD], F32)
        ident = sb("a_ident", [P, P], F32)
        x_in = sb("a_x_in", [P, 2, HID], F32)
        stats = sb("a_stats", [P, 2, 6], F32)
        mean_var = sb("a_mean_var", [P, 2, 2], F32)
        std = sb("a_std", [P, 2, 1], F32)
        rstd = sb("a_rstd", [P, 2, 1], F32)
        eps = sb("a_eps", [P, 1], F32)
        xn = sb("a_xn", [P, 2, HID], F32)
        xn_hi = sb("a_xn_hi", [P, 2, HID], F32R)
        xn_lo = sb("a_xn_lo", [P, 2, HID], F32R)
        by_cos = sb("a_by_cos", [P, 2, QK], F32)
        by_sin = sb("a_by_sin", [P, 2, QK], F32)
        roped = sb("a_roped", [P, 2, QK], F32)
        rest = sb("a_rest", [P, 2, QK], F32)

        xt_ps = ps("a_xt_ps", [P, 2, HID])
        qkv_ps = ps("a_qkv_ps", [P, 2, 1024])
        rt_ps = ps("a_rt_ps", [P, 1024])

        weights_in = [sem(f"a_weights_in{s}") for s in range(2)]
        tables_in = sem("a_tables_in")
        x_loaded = [sem(f"a_x_loaded{s}") for s in range(2)]
        pool_const = sem("a_pool_const")
        ones_set = sem("a_ones_set")
        stack_ones_set = sem("a_stack_ones_set")
        mask_set = sem("a_mask_set")
        ident_set = sem("a_ident_set")
        w_hi_ready = sem("a_w_hi_ready")
        w_lo_ready = sem("a_w_lo_ready")
        stats_done = sem("a_stats_done")
        var_done = sem("a_var_done")
        std_done = sem("a_std_done")
        rstd_done = sem("a_rstd_done")
        xn_done = sem("a_xn_done")
        xt_done = sem("a_xt_done")
        xn_hi_done = sem("a_xn_hi_done")
        passed = sem("a_passed")
        xn_lo_done = sem("a_xn_lo_done")
        qkv_done = sem("a_qkv_done")
        cos_done = sem("a_cos_done")
        sin_done = sem("a_sin_done")
        v_done = sem("a_v_done")
        roped_done = sem("a_roped_done")
        rt_done = sem("a_rt_done")
        part0_done = sem("a_part0_done")
        rest_done = sem("a_rest_done")
        part1_done = sem("a_part1_done")
        part2_done = sem("a_part2_done")

        block = ctx.enter_context(nc.Block())

        def tok(t):
            return bass.ds(t * P, P)

        def store(engine, b):
            for done in (part0_done, part1_done, part2_done):
                engine.wait_ge(done, ST * (b + 1))
            for m in range(PARTS):
                at = bass.ds(b * SEQ, SEQ)
                engine.dma_start(q_parts[m, b * QROWS:(b + 1) * QROWS, :].rearrange("(c p) t -> p c t", p=P),
                                 parts[:, m, 0:QROWS // P, at]).then_inc(parts_out[b], 16)
                engine.dma_start(k_parts[m, b * KROWS:(b + 1) * KROWS, :],
                                 parts[:, m, QROWS // P, at]).then_inc(parts_out[b], 16)

        @block.sync
        def _(sp):
            sp.dma_start(x_in[:, 0, :], x[0:P, :]).then_inc(x_loaded[0], 16)
            sp.dma_start(x_in[:, 1, :], x[P:2 * P, :]).then_inc(x_loaded[1], 16)
            for k in range(KT):
                wait(sp, w_lo_ready, k - 1)
                sp.dma_start(w_raw[:, k % 2, :], wqkv_t[k * P:(k + 1) * P, :]).then_inc(weights_in[k % 2], 16)
            for b in range(BATCH):
                sp.dma_start(cos[:, b * ST:(b + 1) * ST, :], cos_t.rearrange("(t p) d -> p t d", p=P)).then_inc(tables_in, 16)
                sp.dma_start(sin[:, b * ST:(b + 1) * ST, :], sin_t.rearrange("(t p) d -> p t d", p=P)).then_inc(tables_in, 16)

            def load(t, s):
                sp.wait_ge(xn_done, t - 1)
                sp.dma_start(x_in[:, s, :], x[tok(t), :]).then_inc(x_loaded[s], 16)

            early = ST // 2 + 3
            with sp.Fori(1, early) as pair:
                load(2 * pair, 0)
                load(2 * pair + 1, 1)
            store(sp, 0)
            for t in range(2 * early, TT):
                load(t, t % 2)
            sp.wait_ge(parts_out[0], 16 * 2 * PARTS)
            sp.wait_ge(ones_set, 1)
            sp.wait_ge(v_done, ST)
            for n in range(2):
                for_b.load(sp, n, n, q_parts, k_parts)
            store(sp, 1)

        @block.gpsimd
        def _(pool):
            identity(pool, pool_const, ident, 0)
            pool.memset(eps[:, :], EPS).then_inc(pool_const, 1)
            pool.memset(v_all[:, :, :, :], 1.0).then_inc(ones_set, 1)
            pool.wait_ge(ones_set, 1)
            for_b.constants(pool, stack_ones_set, mask_set, ident_set)

            def add(t, s):
                pool.wait_ge(cos_done, t + 1)
                pool.wait_ge(sin_done, 2 * t + 2)
                wait(pool, rt_done, t - 1)
                pool.tensor_tensor(roped[:, s, :], by_cos[:, s, :], by_sin[:, s, :], ALU.add).then_inc(roped_done, 1)

            def last_part(t, s):
                pool.wait_ge(part1_done, t + 1)
                pool.tensor_tensor(parts[:, 2, :, tok(t)], rest[:, s, :].rearrange("p (c t) -> p c t", c=QKT),
                                   parts[:, 1, :, tok(t)], ALU.subtract).then_inc(part2_done, 1)

            def step(t, s):
                if exists(t - 2):
                    last_part(t - 2, s)
                if exists(t):
                    add(t, s)

            over_tiles(pool, step)

        @block.scalar
        def _(act):
            def std_of(t, s):
                act.wait_ge(var_done, t + 1)
                wait(act, rstd_done, t - 1)
                act.activation(std[:, s, :], mean_var[:, s, 1:2], ACT.Sqrt, bias=eps[:, :]).then_inc(std_done, 1)

            def hi(t, s):
                act.wait_ge(xt_done, t + 1)
                wait(act, qkv_done, t - 1)
                act.activation(xn_hi[:, s, :], xt_ps[:, s, :], ACT.Copy).then_inc(xn_hi_done, 1)

            def values(t, s):
                act.wait_ge(sin_done, 2 * t + 2)
                src = qkv_ps[:, s, QK:QKV].rearrange("p (g d) -> p g d", d=HD)
                act.activation(v_all[:, bass.ds(group_row(t), NKV), tile_of(t), 0:HD], src, ACT.Copy).then_inc(v_done, 1)

            def group_row(t):
                return (t // ST) * NKV

            def tile_of(t):
                return t % ST

            def first_parts(t, s):
                act.wait_ge(rt_done, t + 1)
                act.activation(parts[:, 0, :, tok(t)], rt_ps[:, 0:QK].rearrange("p (c t) -> p c t", c=QKT),
                               ACT.Copy).then_inc(part0_done, 1)

            def second_part(t, s):
                act.wait_ge(rest_done, t + 1)
                act.activation(parts[:, 1, :, tok(t)], rest[:, s, :].rearrange("p (c t) -> p c t", c=QKT),
                               ACT.Copy).then_inc(part1_done, 1)

            def step(t, s):
                if exists(t + 1):
                    hi(t + 1, 1 - s)
                if exists(t - 2):
                    first_parts(t - 2, s)
                if exists(t + 2):
                    std_of(t + 2, s)
                if isinstance(t, int) and t == -2:
                    for k in range(KT):
                        act.wait_ge(weights_in[k % 2], 16 * (k // 2 + 1))
                        act.activation(w_hi[:, k, :], w_raw[:, k % 2, :], ACT.Copy).then_inc(w_hi_ready, 1)
                if exists(t - 2):
                    second_part(t - 2, s)
                if exists(t - 1):
                    values(t - 1, 1 - s)

            act.wait_ge(pool_const, 3)
            act.wait_ge(ones_set, 1)
            over_tiles(act, step)

        @block.vector
        def _(dve):
            def first_moments(t, s):
                if isinstance(t, int):
                    dve.wait_ge(x_loaded[s], 16 * (t // 2 + 1))
                else:
                    dve.wait_ge(x_loaded[s], 8 * (t - s) + 16)
                wait(dve, std_done, t - 1)
                wait(dve, xn_done, t - 1)
                dve.bn_stats(stats[:, s, :], x_in[:, s, :]).then_inc(stats_done, 1)

            def moments(t, s):
                wait_apart(dve, stats_done, t + 1, passed)
                dve.bn_aggr(mean_var[:, s, :], stats[:, s, :]).then_inc(var_done, 1)

            def normalise(t, s):
                dve.wait_ge(std_done, t + 1)
                dve.reciprocal(rstd[:, s, :], std[:, s, :]).then_inc(rstd_done, 1)
                dve.wait_ge(rstd_done, t + 1)
                wait(dve, xt_done, t - 1)
                dve.tensor_scalar(xn[:, s, :], x_in[:, s, :], mean_var[:, s, 0:1], rstd[:, s, :],
                                  ALU.subtract, ALU.mult).then_inc(xn_done, 1)

            def lo(t, s):
                dve.wait_ge(xn_hi_done, t + 1)
                dve.tensor_tensor(xn_lo[:, s, :], xt_ps[:, s, :], xn_hi[:, s, :].bitcast(F32),
                                  ALU.subtract).then_inc(xn_lo_done, 1)

            def rotate(t, s):
                dve.wait_ge(qkv_done, t + 1)
                wait(dve, roped_done, t - 1)
                heads = qkv_ps[:, s, 0:QK].rearrange("p (h d) -> p h d", d=HD)
                n = NH + NKV
                dve.tensor_tensor(by_cos[:, s, :].rearrange("p (h d) -> p h d", d=HD), heads,
                                  cos[:, bass.ds(t, 1), :].to_broadcast([P, n, HD]),
                                  ALU.mult).then_inc(cos_done, 1)
                to = by_sin[:, s, :].rearrange("p (h d) -> p h d", d=HD)
                half = HD // 2
                for a, b in ((0, half), (half, 0)):
                    dve.tensor_tensor(to[:, :, a:a + half], heads[:, :, b:b + half],
                                      sin[:, bass.ds(t, 1), a:a + half].to_broadcast([P, n, half]),
                                      ALU.mult).then_inc(sin_done, 1)

            def remainder(t, s):
                dve.wait_ge(part0_done, t + 1)
                wait(dve, part2_done, t - 1)
                wait(dve, part1_done, t - 1)
                dve.tensor_tensor(rest[:, s, :].rearrange("p (c t) -> p c t", c=QKT),
                                  rt_ps[:, 0:QK].rearrange("p (c t) -> p c t", c=QKT),
                                  parts[:, 0, :, tok(t)], ALU.subtract).then_inc(rest_done, 1)

            def step(t, s):
                if exists(t + 2):
                    first_moments(t + 2, s)
                if exists(t + 1):
                    lo(t + 1, 1 - s)
                if exists(t + 2):
                    moments(t + 2, s)
                if exists(t - 2):
                    remainder(t - 2, s)
                if exists(t + 2):
                    normalise(t + 2, s)
                if isinstance(t, int) and t == -2:
                    for k in range(KT):
                        dve.wait_ge(w_hi_ready, k + 1)
                        dve.tensor_tensor(w_lo[:, k, :], w_raw[:, k % 2, :], w_hi[:, k, :].bitcast(F32),
                                          ALU.subtract).then_inc(w_lo_ready, 1)
                    dve.wait_ge(tables_in, 64)
                if exists(t):
                    rotate(t, s)

            over_tiles(dve, step)

        @block.tensor
        def _(pe):
            def x_transposes(t, s):
                pe.wait_ge(xn_done, t + 1)
                wait(pe, xn_lo_done, t - 1)
                for k in range(KT):
                    mm = pe.transpose(xt_ps[:, s, k * P:(k + 1) * P], xn[:, s, k * P:(k + 1) * P], ident[:, :])
                mm.then_inc(xt_done, 1)

            def products(t, s):
                pe.wait_ge(xn_hi_done, t + 1)
                pe.wait_ge(xn_lo_done, t + 1)
                wait(pe, v_done, t - 1)
                wait(pe, cos_done, t - 1)
                wait(pe, sin_done, 2 * t - 2)
                for c0, c1 in ((0, QROWS), (QROWS, QKV)):
                    n = 0
                    for k in range(KT):
                        for a, w in ((xn_hi, w_hi), (xn_hi, w_lo), (xn_lo, w_hi)):
                            mm = pe.matmul(qkv_ps[:, s, c0:c1], a[:, s, k * P:(k + 1) * P], w[:, k, c0:c1],
                                           start=(n == 0), stop=(n == 3 * KT - 1))
                            n += 1
                mm.then_inc(qkv_done, 1)

            def r_transposes(t, s):
                pe.wait_ge(roped_done, t + 1)
                wait(pe, rest_done, t)
                for c in range(QKT):
                    mm = pe.transpose(rt_ps[:, c * P:(c + 1) * P], roped[:, s, c * P:(c + 1) * P], ident[:, :])
                mm.then_inc(rt_done, 1)

            def step(t, s):
                if exists(t + 1):
                    x_transposes(t + 1, 1 - s)
                if exists(t - 2):
                    r_transposes(t - 2, s)
                if exists(t):
                    if isinstance(t, int) and t == 0:
                        pe.wait_ge(w_lo_ready, KT)
                    products(t, s)

            pe.wait_ge(pool_const, 2)
            over_tiles(pe, step)


def phase_b(nc, q_parts, k_parts, for_b, wo_t, for_c, o_vals, o_sums, recips):
    UNITS = GH * ST
    AHEAD = 6
    TURN = 2
    SLOTS, LOADS = for_b.SLOTS, for_b.LOADS
    HALF = SEQ // 2
    CHUNKS = [(hf, j) for hf in range(2) for j in range((hf + 1) * ST // 2)]
    NC = len(CHUNKS)
    DIAG = [c for c, (hf, j) in enumerate(CHUNKS) if j * P >= hf * HALF]
    PRING = 4
    ERING = 3
    INVERT_AT = 30

    class At:
        def __init__(self, p, k):
            self.p, self.k = p, k
            self.n, self.slot, self.turn = SLOTS * p + k, k % SLOTS, p + k // SLOTS

        def next(self, by=1):
            return At(self.p, self.k + by)

        def has(self, by=1):
            return not isinstance(self.n, int) or self.n + by < NG

    def start_of(c):
        hf, j = CHUNKS[c]
        q0 = max(hf * HALF, j * P)
        return q0, (hf + 1) * HALF - q0

    def unit_of(u):
        return ST - 1 - u // GH, u % GH

    def banks_of(u):
        wide = unit_of(u)[0] >= ST // 2
        return (2 * (u % 2), 2) if wide else (u % 4, 1)

    def room_at(u):
        b0, nb = banks_of(u)
        for v in range(u - 1, u - UNITS, -1):
            c0, ncb = banks_of(v % UNITS)
            if b0 < c0 + ncb and c0 < b0 + nb:
                return v + 1

    def plan():
        events = [("u", 1, u) for u in range(AHEAD, UNITS)]
        events += [("u", 2, u) for u in range(TURN)] + [("t", 1, 0)] + [("u", 2, u) for u in range(TURN, AHEAD)]
        cost = [P * (unit_of(u)[0] + 1) + 90 if kind == "u" else P for kind, _, u in events]
        work = [start_of(c)[1] + 100 for c in range(NC) for _ in range(GH)]
        out, e, done, made = [], 0, 0, 0
        for wk in work:
            made += wk
            here = []
            while e < len(events) and (done + cost[e] / 2) * sum(work) <= made * sum(cost):
                here.append(events[e])
                done += cost[e]
                e += 1
            out.append(here)
        out[-1] += events[e:]
        return out

    PLAN = plan()
    TURN_AT = next(i for i, here in enumerate(PLAN) if ("t", 1, 0) in here)

    def is_first(g):
        return isinstance(g.n, int) and g.n == 0

    def is_last(g):
        return isinstance(g.n, int) and g.n == NG - 1

    def over_groups(engine, step):
        step(At(0, 0))
        with engine.Fori(0, (NG - 4) // SLOTS) as p:
            for k in range(1, SLOTS + 1):
                step(At(p, k))
        for n in range(NG - 3, NG):
            step(At(n // SLOTS, n % SLOTS))

    with ExitStack() as ctx:
        def sb(name, shape, dt):
            return ctx.enter_context(nc.sbuf_tensor(name, shape, dt))

        def ps(name, shape, dt=F32):
            return ctx.enter_context(nc.psum_tensor(name, shape, dt))

        def sem(name):
            return ctx.enter_context(nc.semaphore(name))

        q_stack, k_stack, v_here = for_b.q_stack, for_b.k_stack, for_b.v_here
        mask, future, ident = for_b.mask, for_b.future, for_b.ident
        stack_in = for_b.stack_in
        sums = Sums(nc, ctx, "b", o_vals, o_sums, recips)
        wo_raw = sb("b_wo_raw", [P, 2, HID], F32)
        probs = sb("b_probs", [P, PRING, GH, HALF], F32)
        masked = sb("b_masked", [P, 4, SEQ], BF16)
        maxima = sb("b_maxima", [P, SLOTS, UNITS], F32)
        max_rest = sb("b_max_rest", [P, 2, UNITS], F32)
        neg_max = sb("b_neg_max", [P, PARTS, UNITS], BF16)
        neg_max_t = sb("b_neg_max_t", [PARTS * UNITS, P], BF16)
        o_sb = [sb(f"b_o_sb{s}", [P, SEQ], F32) for s in range(SLOTS)]

        max_ps = ps("b_max_ps", [P, 2 * SEQ])
        exp_ps = ps("b_exp_ps", [P, ERING, HALF])
        o_ps = ps("b_o_ps", [P, HALF])
        turn_ps = max_ps[0:PARTS * UNITS, 0:P // 2].bitcast(BF16)

        scores_max = sem("b_scores_max")
        max_read = sem("b_max_read")
        neg_done = sem("b_neg_done")
        turned = sem("b_turned")
        turn_copied = sem("b_turn_copied")
        neg_in = sem("b_neg_in")
        scores_exp = sem("b_scores_exp")
        exp_done = sem("b_exp_done")
        pv_done = sem("b_pv_done")
        o_copied = sem("b_o_copied")
        wo_loaded = [sem(f"b_wo_loaded{s}") for s in range(2)]
        wo_hi_ready = sem("b_wo_hi_ready")
        wo_lo_ready = sem("b_wo_lo_ready")
        dve_passed = sem("b_dve_passed")
        pool_passed = sem("b_pool_passed")
        o_free = sem("b_o_free")

        block = ctx.enter_context(nc.Block())
        SPLIT = 5

        @block.sync
        def _(sp):
            def neg_rows(g):
                sp.wait_ge(turn_copied, g.n + 1)
                for m in range(PARTS):
                    sp.dma_start(q_stack[g.slot][STACK + m:STACK + m + 1, :, :].rearrange("m h (i t) -> m (h i) t", t=P),
                                 neg_max_t[m * UNITS:(m + 1) * UNITS, :]).then_inc(neg_in, 16)

            def step(g):
                last = g.next(-1)
                if not is_first(g):
                    sp.wait_ge(o_copied, 2 * g.n)
                    sums.send(sp, o_sb[last.slot], last.n, last.n)
                if g.has(2):
                    wait(sp, pv_done, NC * g.n)
                    g2 = g.next(2)
                    for_b.load(sp, g2.n, g2.slot, q_parts, k_parts)
                if g.has(1):
                    neg_rows(g.next(1))
                if not is_first(g):
                    sums.send_inverted(sp, last.n, last.n)
                    sums.fetch_factors(sp, last.n, last.n)

            neg_rows(At(0, 0))
            sp.wait_ge(for_b.parts_out[1], 16 * 2 * PARTS)
            over_groups(sp, step)
            sp.wait_ge(o_free, SLOTS - 1 + NG - 1)
            for t in range(2):
                for_c.load(sp, o_vals, t, t)

        @block.gpsimd
        def _(pool):
            def split(g):
                mx, rs, ng = maxima[:, g.slot, :], max_rest, neg_max
                base = SPLIT * g.n
                pool.wait_ge(max_read, UNITS * (g.n + 1))
                wait_apart(pool, turned, g.n, pool_passed)
                pool.tensor_scalar(ng[:, 0, :], mx, -1.0, None, ALU.mult).then_inc(neg_done, 1)
                wait_apart(pool, neg_done, base + 1, pool_passed)
                pool.tensor_tensor(rs[:, 0, :], mx, ng[:, 0, :], ALU.add).then_inc(neg_done, 1)
                wait_apart(pool, neg_done, base + 2, pool_passed)
                pool.tensor_scalar(ng[:, 1, :], rs[:, 0, :], -1.0, None, ALU.mult).then_inc(neg_done, 1)
                wait_apart(pool, neg_done, base + 3, pool_passed)
                pool.tensor_tensor(rs[:, 1, :], rs[:, 0, :], ng[:, 1, :], ALU.add).then_inc(neg_done, 1)
                wait_apart(pool, neg_done, base + 4, pool_passed)
                pool.tensor_scalar(ng[:, 2, :], rs[:, 1, :], -1.0, None, ALU.mult).then_inc(neg_done, 1)

            pool.sem_inc(o_free, SLOTS - 1)
            split(At(0, 0))
            split_weights(pool, [(wo_t[k * P:(k + 1) * P, :], wo_raw[:, k % 2, :], for_c.w_hi[:, k, :], for_c.w_lo[:, k, :])
                                 for k in range(KT)], wo_loaded, wo_hi_ready, wo_lo_ready)

            def step(g):
                if g.has(1):
                    split(g.next(1))
                if not is_first(g):
                    last = g.next(-1)
                    sums.scale(pool, o_sb[last.slot][:, :], last.n)
                    wait_apart(pool, sums.scaled, g.n, pool_passed)
                    sums.store(pool, o_sb[last.slot], last.n)
                    pool.wait_ge(sums.stored, 16 * GH * g.n)
                    pool.sem_inc(o_free, 1)

            over_groups(pool, step)

        @block.scalar
        def _(act):
            def copy_turn(g):
                act.wait_ge(turned, g.n + 1)
                wait(act, neg_in, 16 * PARTS * g.n)
                act.activation(neg_max_t[:, :], turn_ps, ACT.Copy).then_inc(turn_copied, 1)

            def copy_o(g, hf):
                act.wait_ge(pv_done, NC * g.n + (NC if hf else ST // 2))
                wait(act, o_free, g.n)
                o = for_c.o_last if is_last(g) else o_sb[g.slot]
                act.activation(o[:, hf * HALF:(hf + 1) * HALF], o_ps[:, :], ACT.Copy).then_inc(o_copied, 1)

            def step(g):
                for c in range(NC):
                    q0, w = start_of(c)
                    for h in range(GH):
                        i = c * GH + h
                        act.wait_ge(scores_exp, GH * NC * g.n + i + 1)
                        if h == 0:
                            wait(act, pv_done, NC * g.n + c - PRING + 1)
                        if i == TURN_AT and g.has(1):
                            copy_turn(g.next(1))
                        act.activation(probs[:, c % PRING, h, 0:w], exp_ps[:, i % ERING, 0:w], ACT.Exp,
                                       scale=SCALE).then_inc(exp_done, 1)
                    if c == 1 and not (isinstance(g.n, int) and g.n == 0):
                        copy_o(g.next(-1), 1)
                    if c == ST // 2 + 1:
                        copy_o(g, 0)

            copy_turn(At(0, 0))
            over_groups(act, step)
            copy_o(At(0, NG - 1), 1)

        @block.vector
        def _(dve):

            def unit(g, u):
                i, h = unit_of(u)
                w = P * (i + 1)
                b0 = HALF * banks_of(u)[0]
                dve.wait_ge(scores_max, UNITS * g.n + u + 1)
                wait_apart(dve, max_read, UNITS * g.n + u - 3, dve_passed)
                dve.tensor_tensor_reduce(masked[:, u % 4, 0:w], max_ps[:, b0:b0 + w], mask[:, SEQ - w:], 1.0, NEG,
                                         ALU.add, ALU.max, maxima[:, g.slot, h * ST + i:h * ST + i + 1]).then_inc(max_read, 1)

            for u in range(UNITS):
                unit(At(0, 0), u)
            for u in range(AHEAD):
                unit(At(0, 1), u)

            def step(g):
                for i, here in enumerate(PLAN):
                    if i == INVERT_AT and not is_first(g):
                        sums.invert(dve, g.next(-1).n)
                    for kind, by, u in here:
                        if kind == "u" and g.has(by):
                            unit(g.next(by), u)

            over_groups(dve, step)

        @block.tensor
        def _(pe):
            def stacked(g):
                pe.wait_ge(stack_in[g.slot], 16 * LOADS * (g.turn + 1))

            def max_scores(g, u):
                i, h = unit_of(u)
                if u == 0:
                    stacked(g)
                wait(pe, max_read, UNITS * g.n + room_at(u))
                if u == TURN:
                    wait(pe, turn_copied, g.n)
                w = P * (i + 1)
                b0 = HALF * banks_of(u)[0]
                for k0 in range(0, w, HALF):
                    n = min(HALF, w - k0)
                    mm = pe.matmul(max_ps[:, b0 + k0:b0 + k0 + n], q_stack[g.slot][0:STACK, h, i * P:(i + 1) * P],
                                   k_stack[g.slot][0:STACK, k0:k0 + n], start=True, stop=True)
                mm.then_inc(scores_max, 1)

            def turn(g, after):
                pe.wait_ge(neg_done, SPLIT * (g.n + 1))
                if after is not None:
                    pe.wait_ge(max_read, UNITS * after.n + TURN - 1)
                pe.transpose(turn_ps, neg_max[:, :, :].rearrange("p m u -> p (m u)"), ident[:, :]).then_inc(turned, 1)

            def exp_scores(g, c, h):
                hf, j = CHUNKS[c]
                q0, w = start_of(c)
                i = c * GH + h
                if i == 0:
                    pe.wait_ge(neg_in, 16 * PARTS * (g.n + 1))
                wait(pe, exp_done, GH * NC * g.n + i - ERING + 1)
                mm = pe.matmul(exp_ps[:, i % ERING, 0:w], k_stack[g.slot][0:STACKM, j * P:(j + 1) * P],
                               q_stack[g.slot][0:STACKM, h, q0:q0 + w], start=True, stop=c not in DIAG)
                if c in DIAG:
                    mm = pe.matmul(exp_ps[:, i % ERING, 0:P], ident[:, :], future[:, :], start=False, stop=True)
                mm.then_inc(scores_exp, 1)

            def times_values(g, c):
                hf, j = CHUNKS[c]
                q0, w = start_of(c)
                pe.wait_ge(exp_done, GH * (NC * g.n + c + 1))
                if j == 0:
                    wait(pe, o_copied, 2 * g.n + hf)
                o0 = q0 - hf * HALF
                for h in range(GH):
                    mm = pe.matmul(o_ps[h * 2 * HD:(h + 1) * 2 * HD, o0:o0 + w], v_here[g.slot][:, j, :],
                                   probs[:, c % PRING, h, 0:w], start=(j == 0), stop=(j == (hf + 1) * ST // 2 - 1),
                                   skip_group_check=True)
                mm.then_inc(pv_done, 1)

            def step(g):
                for c in range(NC):
                    for h in range(GH):
                        exp_scores(g, c, h)
                        for kind, by, u in PLAN[c * GH + h]:
                            if kind == "u" and g.has(by):
                                max_scores(g.next(by), u)
                            if kind == "t" and g.has(by):
                                turn(g.next(by), g.next(by + 1) if g.has(by + 1) else None)
                    if c >= 2:
                        times_values(g, c - 2)
                    elif not (isinstance(g.n, int) and g.n == 0):
                        times_values(g.next(-1), NC + c - 2)

            for u in range(UNITS):
                max_scores(At(0, 0), u)
            for u in range(TURN):
                max_scores(At(0, 1), u)
            turn(At(0, 0), At(0, 1))
            for u in range(TURN, AHEAD):
                max_scores(At(0, 1), u)
            over_groups(pe, step)
            times_values(At(0, NG - 1), NC - 2)
            times_values(At(0, NG - 1), NC - 1)


def split_weights(pool, pieces, loaded, hi_ready, lo_ready):
    def load(k):
        wait(pool, lo_ready, k - 1)
        pool.dma_start(pieces[k][1], pieces[k][0]).then_inc(loaded[k % 2], 16)

    load(0)
    for k, (_, raw, hi, lo) in enumerate(pieces):
        if k + 1 < len(pieces):
            load(k + 1)
        pool.wait_ge(loaded[k % 2], 16 * (k // 2 + 1))
        pool.tensor_copy(hi, raw).then_inc(hi_ready, 1)
        pool.wait_ge(hi_ready, k + 1)
        pool.tensor_tensor(lo, raw, hi.bitcast(F32), ALU.subtract).then_inc(lo_ready, 1)


def phase_c(nc, x, o_vals, o_sums, recips, x1, xn_t, wgu_t, for_c, for_d):
    XRING = 4
    with ExitStack() as ctx:
        def sb(name, shape, dt):
            return ctx.enter_context(nc.sbuf_tensor(name, shape, dt))

        def ps(name, shape):
            return ctx.enter_context(nc.psum_tensor(name, shape, F32))

        def sem(name):
            return ctx.enter_context(nc.semaphore(name))

        w_hi, w_lo, o_in, o_loaded, o_last = for_c.w_hi, for_c.w_lo, for_c.o_in, for_c.o_loaded, for_c.o_last
        up_hi, up_lo = for_d.up_hi, for_d.up_lo
        ident = sb("c_ident", [P, P], F32)
        eps = sb("c_eps", [P, 1], F32)
        sums = Sums(nc, ctx, "c", o_vals, o_sums, recips)
        up_raw = sb("c_up_raw", [P, 2, INTER], F32)
        x_in = sb("c_x_in", [P, XRING, HID], F32)
        attn_hi = sb("c_attn_hi", [P, 2, KT, P], F32R)
        attn_lo = sb("c_attn_lo", [P, 2, KT, P], F32R)
        x1_sb = sb("c_x1_sb", [P, 2, HID], F32)
        stats = sb("c_stats", [P, 2, 6], F32)
        mean_var = sb("c_mean_var", [P, 2, 2], F32)
        std = sb("c_std", [P, 2, 1], F32)
        rstd = sb("c_rstd", [P, 2, 1], F32)
        xn = sb("c_xn", [P, 2, HID], F32)
        xt_sb = sb("c_xt_sb", [P, 2, HID], F32)

        y_ps = ps("c_y_ps", [P, 2, HID])
        xt_ps = ps("c_xt_ps", [P, 2, HID])

        x_loaded = [sem(f"c_x_loaded{s}") for s in range(2)]
        x1_stored = [sem(f"c_x1_stored{s}") for s in range(2)]
        xt_stored = [sem(f"c_xt_stored{s}") for s in range(2)]
        pool_const = sem("c_pool_const")
        up_loaded = sem("c_up_loaded")
        up_hi_ready = sem("c_up_hi_ready")
        up_lo_ready = sem("c_up_lo_ready")
        attn_hi_done = sem("c_attn_hi_done")
        attn_lo_done = sem("c_attn_lo_done")
        y_done = sem("c_y_done")
        x1_done = sem("c_x1_done")
        stats_done = sem("c_stats_done")
        var_done = sem("c_var_done")
        std_done = sem("c_std_done")
        rstd_done = sem("c_rstd_done")
        xn_done = sem("c_xn_done")
        xt_done = sem("c_xt_done")
        xt_copied = sem("c_xt_copied")
        xn_loaded = sem("c_xn_loaded")
        xn_hi_done = sem("c_xn_hi_done")
        xn_lo_done = sem("c_xn_lo_done")
        passed = sem("c_passed")
        sp_passed = sem("c_sp_passed")

        block = ctx.enter_context(nc.Block())

        def tok(t):
            return bass.ds(t * P, P)

        def twice(s, t):
            return 16 * (t // 2 + 1) if isinstance(t, int) else 8 * (t - s) + 16

        def is_last(t, by=0):
            return isinstance(t, int) and t == TT - 1 + by

        def piece(t):
            return t // 2

        def attn(t):
            return o_in[:, bass.ds(t % for_c.RING, 1), :, :].rearrange("p a k t -> p (a k) t")

        def flat(tensor, i):
            return tensor[:, bass.ds(i, 1), :].rearrange("p a n -> p (a n)")

        @block.sync
        def _(sp):
            def load_o(t, s):
                wait_apart(sp, attn_lo_done, t - for_c.RING + 1, sp_passed)
                wait_apart(sp, attn_hi_done, t - 1, sp_passed)
                for_c.load(sp, o_vals, t, s)

            def load_x(t, s):
                wait(sp, x1_done, t - XRING + 1)
                sp.dma_start(flat(x_in, t % XRING), x[tok(t), :]).then_inc(x_loaded[s], 16)

            def load_piece(t):
                q = piece(t)
                wait_apart(sp, up_lo_ready, t - 2, sp_passed)
                wait_apart(sp, up_loaded, 8 * t, sp_passed)
                sp.dma_start(flat(up_raw, q % 2), wgu_t[bass.ds(q * P, P), :]).then_inc(up_loaded, 16)

            def step(t, s):
                if exists(t + 2):
                    if not isinstance(t, int) or t >= 0:
                        load_o(t + 2, s)
                    load_x(t + 2, s)
                if s == 0 and exists(t):
                    load_piece(t)
                if isinstance(t, int) and t == -2:
                    sums.send(sp, o_last, NG - 1, 0)
                if isinstance(t, int) and t == -1:
                    sums.send_inverted(sp, NG - 1, 0)
                if isinstance(t, int) and t == 0:
                    sums.fetch_factors(sp, NG - 1, 0)
                if isinstance(t, int) and t == 3:
                    sp.wait_ge(sums.stored, 16 * GH)
                if is_last(t, -1):
                    for r in range(2):
                        sp.wait_ge(xt_stored[r], 8 * CT)
                    sp.dma_start(for_d.xn_raw[:, :, :], xn_t[:, 0:CW].rearrange("(k p) t -> p k t", p=P)).then_inc(xn_loaded, 16)

            over_tiles(sp, step)
            for s in range(2):
                sp.wait_ge(x1_stored[s], 8 * TT)
                sp.wait_ge(xt_stored[s], 8 * TT)

        @block.gpsimd
        def _(pool):
            identity(pool, pool_const, ident, 0)
            pool.memset(eps[:, :], EPS).then_inc(pool_const, 1)

            def piece_lo(t):
                q = piece(t)
                pool.wait_ge(up_hi_ready, t + 2)
                pool.tensor_tensor(flat(up_lo, q), flat(up_raw, q % 2), flat(up_hi, q).bitcast(F32),
                                   ALU.subtract).then_inc(up_lo_ready, 2)

            def step(t, s):
                if isinstance(t, int) and t == 0:
                    sums.scale(pool, o_last[:, :], 0)
                    pool.wait_ge(sums.scaled, 1)
                    sums.store(pool, o_last, NG - 1)
                if s == 0 and exists(t - 2):
                    piece_lo(t - 2)

            over_tiles(pool, step)

        @block.scalar
        def _(act):
            act.wait_ge(pool_const, 3)

            def hi(t, s):
                act.wait_ge(o_loaded[s], twice(s, t))
                wait(act, y_done, t - 1)
                act.activation(attn_hi[:, s, :, :], attn(t), ACT.Copy).then_inc(attn_hi_done, 1)

            def piece_hi(t):
                q = piece(t)
                act.wait_ge(up_loaded, 8 * t + 16)
                act.activation(flat(up_hi, q), flat(up_raw, q % 2), ACT.Copy).then_inc(up_hi_ready, 2)

            def std_of(t, s):
                act.wait_ge(var_done, t + 1)
                wait(act, rstd_done, t - 1)
                act.activation(std[:, s, :], mean_var[:, s, 1:2], ACT.Sqrt, bias=eps[:, :]).then_inc(std_done, 1)

            def out(t, s):
                act.wait_ge(xt_done, t + 1)
                if isinstance(t, int):
                    wait(act, xt_stored[s], 16 * (t // 2))
                else:
                    act.wait_ge(xt_stored[s], 8 * (t - s))
                act.activation(xt_sb[:, s, :], xt_ps[:, s, :], ACT.Copy).then_inc(xt_copied, 1)

            def store_x1(t, s):
                act.wait_ge(x1_done, t + 1)
                act.dma_start(x1[tok(t), :], x1_sb[:, s, :]).then_inc(x1_stored[s], 16)

            def store_xt(t, s):
                act.wait_ge(xt_copied, t + 1)
                act.dma_start(xn_t[:, tok(t)].rearrange("(k p) t -> p k t", p=P),
                              xt_sb[:, s, :].rearrange("p (k t) -> p k t", k=KT)).then_inc(xt_stored[s], 16)

            def step(t, s):
                if exists(t + 1):
                    hi(t + 1, 1 - s)
                if exists(t - 2):
                    out(t - 2, s)
                if exists(t - 1):
                    std_of(t - 1, 1 - s)
                    store_x1(t - 1, 1 - s)
                if exists(t - 2):
                    store_xt(t - 2, s)
                if s == 1 and exists(t - 1):
                    piece_hi(t - 1)
                if is_last(t):
                    act.wait_ge(xn_loaded, 16)
                    for k in range(KT):
                        act.activation(for_d.xn_hi[:, 0, k, :], for_d.xn_raw[:, k, :], ACT.Copy).then_inc(xn_hi_done, 1)

            over_tiles(act, step)

        @block.vector
        def _(dve):
            def lo(t, s):
                dve.wait_ge(attn_hi_done, t + 1)
                wait(dve, y_done, t - 1)
                dve.tensor_tensor(attn_lo[:, s, :, :], attn(t), attn_hi[:, s, :, :].bitcast(F32),
                                  ALU.subtract).then_inc(attn_lo_done, 1)

            def residual(t, s):
                dve.wait_ge(y_done, t + 1)
                dve.wait_ge(x_loaded[s], twice(s, t))
                if isinstance(t, int):
                    wait(dve, x1_stored[s], 16 * (t // 2))
                else:
                    dve.wait_ge(x1_stored[s], 8 * (t - s))
                wait(dve, xn_done, t - 1)
                dve.tensor_tensor(x1_sb[:, s, :], y_ps[:, s, :], flat(x_in, t % XRING), ALU.add).then_inc(x1_done, 1)

            def first_moments(t, s):
                dve.wait_ge(x1_done, t + 1)
                wait(dve, std_done, t - 1)
                dve.bn_stats(stats[:, s, :], x1_sb[:, s, :]).then_inc(stats_done, 1)

            def moments(t, s):
                wait_apart(dve, stats_done, t + 1, passed)
                dve.bn_aggr(mean_var[:, s, :], stats[:, s, :]).then_inc(var_done, 1)

            def normalise(t, s):
                dve.wait_ge(std_done, t + 1)
                dve.reciprocal(rstd[:, s, :], std[:, s, :]).then_inc(rstd_done, 1)
                dve.wait_ge(rstd_done, t + 1)
                wait(dve, xt_done, t - 1)
                dve.tensor_scalar(xn[:, s, :], x1_sb[:, s, :], mean_var[:, s, 0:1], rstd[:, s, :],
                                  ALU.subtract, ALU.mult).then_inc(xn_done, 1)

            def step(t, s):
                if exists(t - 1):
                    residual(t - 1, 1 - s)
                    first_moments(t - 1, 1 - s)
                    moments(t - 1, 1 - s)
                if exists(t + 1):
                    lo(t + 1, 1 - s)
                if exists(t - 1):
                    normalise(t - 1, 1 - s)
                if isinstance(t, int) and t == -1:
                    sums.invert(dve, 0)

            over_tiles(dve, step)
            for k in range(KT):
                dve.wait_ge(xn_hi_done, k + 1)
                dve.tensor_tensor(for_d.xn_lo[:, 0, k, :], for_d.xn_raw[:, k, :], for_d.xn_hi[:, 0, k, :].bitcast(F32),
                                  ALU.subtract).then_inc(xn_lo_done, 1)

        @block.tensor
        def _(pe):
            def products(t, s):
                pe.wait_ge(attn_lo_done, t + 1)
                wait(pe, x1_done, t - 1)
                n = 0
                for k in range(KT):
                    for a, w in ((attn_hi, w_hi), (attn_hi, w_lo), (attn_lo, w_hi)):
                        mm = pe.matmul(y_ps[:, s, :], a[:, s, k, :], w[:, k, :], start=(n == 0), stop=(n == 3 * KT - 1))
                        n += 1
                mm.then_inc(y_done, 1)

            def x_transposes(t, s):
                pe.wait_ge(xn_done, t + 1)
                wait(pe, xt_copied, t - 1)
                for k in range(KT):
                    mm = pe.transpose(xt_ps[:, s, k * P:(k + 1) * P], xn[:, s, k * P:(k + 1) * P], ident[:, :])
                mm.then_inc(xt_done, 1)

            def step(t, s):
                if exists(t):
                    products(t, s)
                if exists(t - 2):
                    x_transposes(t - 2, s)

            pe.wait_ge(pool_const, 2)
            over_tiles(pe, step)


def phase_d(nc, wd_t, x1, xn_t, out, for_d, from_c):
    NCH = TT // CT
    SPLIT_AT = 4

    def rows(i):
        return min(P, INTER - i * P)

    with ExitStack() as ctx:
        def sb(name, shape, dt):
            return ctx.enter_context(nc.sbuf_tensor(name, shape, dt))

        def ps(name, shape):
            return ctx.enter_context(nc.psum_tensor(name, shape, F32))

        def sem(name):
            return ctx.enter_context(nc.semaphore(name))

        up_hi, up_lo = for_d.up_hi, for_d.up_lo
        xn_raw, xn_hi, xn_lo = for_d.xn_raw, for_d.xn_hi, for_d.xn_lo
        h_hi, h_lo = from_c.w_hi, from_c.w_lo
        gate = from_c.o_in[:, 0:2, :, :].rearrange("p s k t -> p s (k t)")
        wd_raw = from_c.o_in[:, 2:4, :, :].rearrange("p s k t -> p s (k t)")
        prod = from_c.o_last[:, 0:CW]
        wd_hi = sb("d_wd_hi", [P, IT, HID], F32R)
        wd_lo = sb("d_wd_lo", [P, IT, HID], F32R)
        y_sb = sb("d_y_sb", [P, CT, HID], F32)

        g_ps = ps("d_g_ps", [P, 2, CW])
        u_ps = ps("d_u_ps", [P, 2, CW])
        y_ps = ps("d_y_ps", [P, CT, HID])

        wd_loaded = [sem(f"d_wd_loaded{s}") for s in range(2)]
        wd_hi_ready = sem("d_wd_hi_ready")
        wd_lo_ready = sem("d_wd_lo_ready")
        xn_in = sem("d_xn_in")
        x1_loaded = sem("d_x1_loaded")
        xn_hi_done = sem("d_xn_hi_done")
        xn_lo_done = sem("d_xn_lo_done")
        g_done = sem("d_g_done")
        u_done = sem("d_u_done")
        gate_done = sem("d_gate_done")
        prod_done = sem("d_prod_done")
        h_hi_done = sem("d_h_hi_done")
        h_lo_done = sem("d_h_lo_done")
        y_step = sem("d_y_step")
        out_done = sem("d_out_done")
        out_stored = sem("d_out_stored")

        block = ctx.enter_context(nc.Block())

        def over_chunks(engine, chunk):
            chunk(0)
            with engine.Fori(1, NCH - 1) as c:
                chunk(c)
            chunk(NCH - 1)

        def is_first(c):
            return isinstance(c, int) and c == 0

        def has_next(c):
            return not isinstance(c, int) or c + 1 < NCH

        def slot(tensor, c, k):
            if isinstance(c, int):
                return tensor[:, c % 2, k, :]
            return tensor[:, bass.ds(c % 2, 1), k, :].rearrange("p a t -> p (a t)")

        def two_back(n, i):
            return n if i == 0 and IT % 2 else n - 1

        @block.sync
        def _(sp):
            def load_xn(c):
                wait(sp, xn_lo_done, KT * (c - 1))
                sp.dma_start(xn_raw[:, :, :], xn_t[:, bass.ds(c * CW, CW)].rearrange("(k p) t -> p k t", p=P)).then_inc(xn_in, 16)

            def load_x1(c):
                wait(sp, out_stored, 16 * CT * c)
                sp.dma_start(y_sb[:, :, :], x1[bass.ds(c * CW, CW), :].rearrange("(a p) n -> p a n", p=P)).then_inc(x1_loaded, 16)

            def store(c):
                for a in range(CT):
                    sp.wait_ge(out_done, CT * c + a + 1)
                    sp.dma_start(out[bass.ds(c * CW + a * P, P), :], y_sb[:, a, :]).then_inc(out_stored, 16)

            def chunk(c):
                if has_next(c):
                    load_xn(c + 1)
                if not is_first(c):
                    store(c - 1)
                load_x1(c)

            over_chunks(sp, chunk)
            store(NCH - 1)
            sp.wait_ge(out_stored, 16 * CT * NCH)

        @block.gpsimd
        def _(pool):
            split_weights(pool, [(wd_t[i * P:i * P + rows(i), :], wd_raw[0:rows(i), i % 2, :],
                                  wd_hi[0:rows(i), i, :], wd_lo[0:rows(i), i, :]) for i in range(IT)],
                          wd_loaded, wd_hi_ready, wd_lo_ready)

        @block.scalar
        def _(act):
            def split_xn(c, k):
                act.wait_ge(xn_in, 16 * c)
                wait(act, u_done, IT * (c - 1))
                act.activation(slot(xn_hi, c, k), xn_raw[:, k, :], ACT.Copy).then_inc(xn_hi_done, 1)

            def silu(c, i):
                n = IT * c + i
                r = rows(i)
                act.wait_ge(g_done, n + 1)
                wait(act, prod_done, two_back(n, i))
                act.activation(gate[0:r, i % 2, :], g_ps[0:r, i % 2, :], ACT.Silu).then_inc(gate_done, 1)

            def hi(c, i):
                n = IT * c + i
                r = rows(i)
                act.wait_ge(prod_done, n + 1)
                wait(act, y_step, two_back(n, i))
                act.activation(h_hi[0:r, i % 2, :], prod[0:r, :], ACT.Copy).then_inc(h_hi_done, 1)

            def chunk(c):
                for i in range(IT):
                    silu(c, i)
                    if i >= 1:
                        hi(c, i - 1)
                    elif not is_first(c):
                        hi(c - 1, IT - 1)
                    if has_next(c) and 0 <= i - SPLIT_AT < KT:
                        split_xn(c + 1, i - SPLIT_AT)

            over_chunks(act, chunk)
            hi(NCH - 1, IT - 1)

        @block.vector
        def _(dve):
            def split_xn(c, k):
                dve.wait_ge(xn_hi_done, KT * (c - 1) + k + 1)
                wait(dve, u_done, IT * (c - 1))
                dve.tensor_tensor(slot(xn_lo, c, k), xn_raw[:, k, :], slot(xn_hi, c, k).bitcast(F32),
                                  ALU.subtract).then_inc(xn_lo_done, 1)

            def product(c, i):
                n = IT * c + i
                r = rows(i)
                dve.wait_ge(gate_done, n + 1)
                dve.wait_ge(u_done, n + 1)
                wait(dve, h_lo_done, n)
                dve.tensor_tensor(prod[0:r, :], u_ps[0:r, i % 2, :], gate[0:r, i % 2, :], ALU.mult).then_inc(prod_done, 1)

            def lo(c, i):
                n = IT * c + i
                r = rows(i)
                dve.wait_ge(h_hi_done, n + 1)
                wait(dve, y_step, two_back(n, i))
                dve.tensor_tensor(h_lo[0:r, i % 2, :], prod[0:r, :], h_hi[0:r, i % 2, :].bitcast(F32),
                                  ALU.subtract).then_inc(h_lo_done, 1)

            def add(c):
                dve.wait_ge(x1_loaded, 16 * (c + 1))
                dve.wait_ge(y_step, IT * (c + 1))
                for a in range(CT):
                    dve.tensor_tensor(y_sb[:, a, :], y_ps[:, a, :], y_sb[:, a, :], ALU.add).then_inc(out_done, 1)

            def chunk(c):
                for i in range(IT):
                    product(c, i)
                    if i == 0 and not is_first(c):
                        add(c - 1)
                    lo(c, i)
                    if has_next(c) and 0 <= i - SPLIT_AT < KT:
                        split_xn(c + 1, i - SPLIT_AT)

            over_chunks(dve, chunk)
            add(NCH - 1)

        @block.tensor
        def _(pe):
            def up(c, i, w, bank, done):
                r = rows(i)
                n = 0
                for k in range(KT):
                    cols = slice(i * P, i * P + r)
                    if i == 0:
                        wait(pe, xn_lo_done, 0 if is_first(c) else KT * (c - 1) + k + 1)
                    for a, b in ((up_hi, xn_hi), (up_hi, xn_lo), (up_lo, xn_hi)):
                        mm = pe.matmul(bank[0:r, i % 2, :], a[:, KT * w + k, cols], slot(b, c, k), start=(n == 0), stop=(n == 3 * KT - 1))
                        n += 1
                mm.then_inc(done, 1)

            def down(c, i):
                r = rows(i)
                pe.wait_ge(h_lo_done, IT * c + i + 1)
                if is_first(c) or i == IT - 1:
                    pe.wait_ge(wd_lo_ready, i + 1)
                if i == 0:
                    wait(pe, out_done, CT * c)
                for a in range(CT):
                    toks = slice(a * P, (a + 1) * P)
                    for n, (h, w) in enumerate(((h_hi, wd_hi), (h_hi, wd_lo), (h_lo, wd_hi))):
                        mm = pe.matmul(y_ps[:, a, :], h[0:r, i % 2, toks], w[0:r, i, :],
                                       start=(i == 0 and n == 0), stop=(i == IT - 1 and n == 2))
                mm.then_inc(y_step, 1)

            def chunk(c):
                for i in range(IT):
                    wait(pe, prod_done, two_back(IT * c + i, i))
                    up(c, i, 0, g_ps, g_done)
                    up(c, i, 1, u_ps, u_done)
                    if i >= 1:
                        down(c, i - 1)
                    elif not is_first(c):
                        down(c - 1, IT - 1)

            over_chunks(pe, chunk)
            down(NCH - 1, IT - 1)


def transformer_layer(nc, x, wqkv_t, wo_t, wgu_t, wd_t, cos_t, sin_t, out):
    q_parts = nc.dram_tensor("q_parts", [PARTS, BATCH * QROWS, SEQ], BF16, kind="Internal").ap()
    k_parts = nc.dram_tensor("k_parts", [PARTS, BATCH * KROWS, SEQ], BF16, kind="Internal").ap()
    o_vals = nc.dram_tensor("o_vals", [NG, GH * HD, SEQ], F32, kind="Internal").ap()
    o_sums = nc.dram_tensor("o_sums", [NG, GH, SEQ], F32, kind="Internal").ap()
    recips = nc.dram_tensor("recips", [NG, GH, SEQ], F32, kind="Internal").ap()
    x1 = nc.dram_tensor("x1", [TOK, HID], F32, kind="Internal").ap()
    xn_t = nc.dram_tensor("xn_t", [HID, TOK], F32, kind="Internal").ap()
    with ExitStack() as until_d:
        for_c = ForC(nc, until_d)
        with ExitStack() as until_b:
            for_b = ForB(nc, until_b)
            phase_a(nc, x, wqkv_t, cos_t, sin_t, q_parts, k_parts, for_b, for_c)
            phase_b(nc, q_parts, k_parts, for_b, wo_t, for_c, o_vals, o_sums, recips)
        for_d = ForD(nc, until_d)
        phase_c(nc, x, o_vals, o_sums, recips, x1, xn_t, wgu_t, for_c, for_d)
        phase_d(nc, wd_t, x1, xn_t, out, for_d, for_c)


def kernel(L0_attn_hidden_states, L0_attn_Wq, L0_attn_Wk, L0_attn_Wv, L0_attn_Wo, L0_ffn_w_gate, L0_ffn_w_up,
           L0_ffn_w_down):
    import numpy as np
    import concourse.bacc as bacc
    from concourse.bass_utils import run_bass_kernel_spmd

    inv_freq = (1.0 / np.float32(10000.0) ** (np.arange(0, HD, 2, dtype=np.float32) / np.float32(HD))).astype(np.float32)
    angle = np.outer(np.arange(SEQ, dtype=np.float32), inv_freq).astype(np.float32)
    cos_t = np.concatenate([np.cos(angle), np.cos(angle)], axis=1).astype(np.float32)
    sin_t = np.concatenate([-np.sin(angle), np.sin(angle)], axis=1).astype(np.float32)

    def turned(w):
        return np.ascontiguousarray(np.asarray(w).T)

    arrays = {
        "x": np.ascontiguousarray(np.asarray(L0_attn_hidden_states).reshape(TOK, HID)),
        "wqkv_t": turned(np.concatenate([np.asarray(L0_attn_Wq), np.asarray(L0_attn_Wk), np.asarray(L0_attn_Wv)], axis=0)),
        "wo_t": turned(L0_attn_Wo),
        "wgu_t": np.concatenate([turned(L0_ffn_w_gate), turned(L0_ffn_w_up)], axis=0),
        "wd_t": turned(L0_ffn_w_down),
        "cos_t": cos_t,
        "sin_t": sin_t,
    }
    nc = bacc.Bacc("TRN2", target_bir_lowering=False, num_devices=1)
    args = [nc.dram_tensor(f"in_{name}", a.shape, mybir.dt.from_np(a.dtype), kind="ExternalInput").ap()
            for name, a in arrays.items()]
    out = nc.dram_tensor("out_0", (TOK, HID), F32, kind="ExternalOutput").ap()
    transformer_layer(nc, *args, out)
    r = run_bass_kernel_spmd(nc, [{f"in_{name}": a for name, a in arrays.items()}], core_ids=[0])
    return r.results[0]["out_0"].reshape(BATCH, SEQ, HID)
```
